# Optimizing a Trainium2 kernel written in Bass

```python
import numpy as np
import jax
import jax.numpy as jnp

def _softmax(x, axis=-1):
    return jax.nn.softmax(x, axis=axis)

def _gelu(x):
    return jax.nn.gelu(x, approximate=True)

def _silu(x):
    return jax.nn.silu(x)

def _sigmoid(x):
    return jax.nn.sigmoid(x)

def _layernorm(x, axis=-1, eps=1e-05):
    m = jnp.mean(x, axis=axis, keepdims=True)
    v = jnp.var(x, axis=axis, keepdims=True)
    return (x - m) / jnp.sqrt(v + eps)

def _scatter_add(tgt, idx, src, axis=0):
    return tgt.at[idx].add(src)

def _segment_sum(src, seg, n):
    return jax.ops.segment_sum(src, seg, n)
kernel_name = 'mk_gnn_preln_d4_gnn_r16_cf5529'

def setup_inputs(seed: int=0):
    np.random.seed(seed)
    _w = jnp.asarray

    def _rec_inputs():
        import jax
        import jax.numpy as jnp
        _gk = jax.random.key(seed)
        x = -0.0003713 + 1 * jax.random.normal(jax.random.fold_in(_gk, 1), (3125, 256), jnp.float32)
        src = jax.random.randint(jax.random.fold_in(_gk, 2), (100000,), 0, 3125, jnp.int32)
        dst = jax.random.randint(jax.random.fold_in(_gk, 3), (100000,), 0, 3125, jnp.int32)
        _o = jnp.argsort(dst, stable=True)
        src = src[_o]
        dst = dst[_o]
        edge_attr_64 = 0.000283511 + 1.00007 * jax.random.normal(jax.random.fold_in(_gk, 12), (100000, 64), jnp.float32)
        edge_weight = jax.random.uniform(jax.random.fold_in(_gk, 14), (100000,), jnp.float32, 0.0, 1)
        return (x, src, dst, edge_attr_64, edge_weight)
    x, src, dst, edge_attr_64, edge_weight = _rec_inputs()

    def _L0_gnn_setup():
        import jax, jax.numpy as jnp
        import numpy as np
        N, E = (3125, 50000)
        NFEAT, NHID, NCLASS, HEADS = (256, 256, 64, 4)
        NEG_SLOPE = 0.2

        def gat_conv(x, src, dst, W, a_src, a_dst, b):
            H, C = a_src.shape
            h = (x @ W).reshape(-1, H, C)
            alpha_s = jnp.einsum('nhc,hc->nh', h, a_src)
            alpha_d = jnp.einsum('nhc,hc->nh', h, a_dst)
            e = jax.nn.leaky_relu(alpha_s[src] + alpha_d[dst], NEG_SLOPE)
            m = jax.ops.segment_max(e, dst, num_segments=N)
            ex = jnp.exp(e - m[dst])
            s = jax.ops.segment_sum(ex, dst, num_segments=N)
            alpha = ex / (s[dst] + 1e-16)
            out = jax.ops.segment_sum(h[src] * alpha[:, :, None], dst, num_segments=N)
            return out.reshape(-1, H * C) + b
        key = jax.random.key(seed)
        ks = jax.random.split(key, 12)
        glorot = lambda k, shape: jax.random.normal(k, shape, jnp.float32) * jnp.sqrt(2.0 / (shape[0] + shape[-1]))
        x = jax.random.normal(ks[0], (N, NFEAT), jnp.float32)
        edge_index = jax.random.randint(ks[1], (2, E), 0, N, jnp.int64)
        W1 = glorot(ks[2], (NFEAT, HEADS * NCLASS))
        att_src1 = glorot(ks[3], (HEADS, NCLASS))
        att_dst1 = glorot(ks[4], (HEADS, NCLASS))
        b1 = jnp.zeros((HEADS * NCLASS,), jnp.float32)
        W2 = glorot(ks[5], (NHID, HEADS * NCLASS))
        att_src2 = glorot(ks[6], (HEADS, NCLASS))
        att_dst2 = glorot(ks[7], (HEADS, NCLASS))
        b2 = jnp.zeros((HEADS * NCLASS,), jnp.float32)
        return {'x': x, 'edge_index': edge_index, 'W1': W1, 'att_src1': att_src1, 'att_dst1': att_dst1, 'b1': b1, 'W2': W2, 'att_src2': att_src2, 'att_dst2': att_dst2, 'b2': b2}
    _L0_gnn_all = _L0_gnn_setup()
    _L0_gnn_in = {k: v for k, v in _L0_gnn_all.items() if k in ('W1', 'att_src1', 'att_dst1', 'b1', 'W2', 'att_src2', 'att_dst2', 'b2')}
    del _L0_gnn_all

    def _L1_gnn_setup():
        import jax, jax.numpy as jnp
        import numpy as np
        N_NODES = 3125
        N_EDGES = 50000
        DIM = 256
        HEADS = 8
        DIM_OUT = 32
        key = jax.random.key(seed)
        ks = jax.random.split(key, 9)
        s = 1.0 / np.sqrt(DIM)
        inner = HEADS * DIM_OUT
        return {'x': jax.random.normal(ks[0], (N_NODES, DIM), dtype=jnp.float32), 'Wq': jax.random.uniform(ks[1], (DIM, inner), jnp.float32, -s, s), 'bq': jax.random.uniform(ks[2], (inner,), jnp.float32, -s, s), 'Wk': jax.random.uniform(ks[3], (DIM, inner), jnp.float32, -s, s), 'bk': jax.random.uniform(ks[4], (inner,), jnp.float32, -s, s), 'Wv': jax.random.uniform(ks[5], (DIM, inner), jnp.float32, -s, s), 'bv': jax.random.uniform(ks[6], (inner,), jnp.float32, -s, s), 'src': jax.random.randint(ks[7], (N_EDGES,), 0, N_NODES), 'dst': jax.random.randint(ks[8], (N_EDGES,), 0, N_NODES)}
    _L1_gnn_all = _L1_gnn_setup()
    _L1_gnn_in = {k: v for k, v in _L1_gnn_all.items() if k in ('Wq', 'bq', 'Wk', 'bk', 'Wv', 'bv')}
    del _L1_gnn_all

    def _L2_gnn_setup():
        import jax, jax.numpy as jnp
        import numpy as np
        N_NODES = 25000
        N_EDGES = 18750
        D_NODE = 256
        D_EDGE = 64
        LN_EPS = 0.001
        key = jax.random.key(seed)
        k1, k2, k3, k4 = jax.random.split(key, 4)
        node_features = jax.random.normal(k1, (N_NODES, D_NODE), dtype=jnp.float32)
        edge_index = jax.random.randint(k2, (2, N_EDGES), 0, N_NODES, dtype=jnp.int32)
        edge_features = jax.random.normal(k3, (N_EDGES, D_EDGE), dtype=jnp.float32)
        W = jax.random.normal(k4, (D_NODE + D_EDGE, D_NODE), dtype=jnp.float32) * (1.0 / np.sqrt(D_NODE + D_EDGE))
        b = jnp.zeros((D_NODE,), dtype=jnp.float32)
        gamma = jnp.ones((D_NODE,), dtype=jnp.float32)
        beta = jnp.zeros((D_NODE,), dtype=jnp.float32)
        return {'node_features': node_features, 'edge_index': edge_index, 'edge_features': edge_features, 'W': W, 'b': b, 'gamma': gamma, 'beta': beta}
    _L2_gnn_all = _L2_gnn_setup()
    _L2_gnn_in = {k: v for k, v in _L2_gnn_all.items() if k in ('W', 'b', 'gamma', 'beta')}
    del _L2_gnn_all

    def _L3_gnn_setup():
        import jax, jax.numpy as jnp
        import numpy as np
        N_NODES = 3125
        N_EDGES = 50000
        F_IN = 256
        F_OUT = 64
        HEADS = 4
        LEAKY_ALPHA = 0.2
        key = jax.random.key(seed)
        ks = jax.random.split(key, 8)
        x = jax.random.normal(ks[0], (N_NODES, F_IN), dtype=jnp.float32)
        W = jax.random.normal(ks[1], (HEADS, F_IN, F_OUT), dtype=jnp.float32) * 0.05
        a_self = jax.random.normal(ks[2], (HEADS, F_OUT), dtype=jnp.float32) * 0.05
        a_neigh = jax.random.normal(ks[3], (HEADS, F_OUT), dtype=jnp.float32) * 0.05
        bias = jnp.zeros((HEADS, F_OUT), dtype=jnp.float32)
        adj_val = jnp.ones((N_EDGES,), dtype=jnp.float32)
        edge_row = jax.random.randint(ks[4], (N_EDGES,), 0, N_NODES, dtype=jnp.int32)
        edge_col = jax.random.randint(ks[5], (N_EDGES,), 0, N_NODES, dtype=jnp.int32)
        return {'x': x, 'W': W, 'a_self': a_self, 'a_neigh': a_neigh, 'bias': bias, 'adj_val': adj_val, 'edge_row': edge_row, 'edge_col': edge_col}
    _L3_gnn_all = _L3_gnn_setup()
    _L3_gnn_in = {k: v for k, v in _L3_gnn_all.items() if k in ('W', 'a_self', 'a_neigh', 'bias')}
    del _L3_gnn_all
    return {'x': x, 'src': src, 'dst': dst, 'edge_attr_64': edge_attr_64, 'edge_weight': edge_weight, 'L0_gnn_W1': _L0_gnn_in['W1'], 'L0_gnn_att_src1': _L0_gnn_in['att_src1'], 'L0_gnn_att_dst1': _L0_gnn_in['att_dst1'], 'L0_gnn_b1': _L0_gnn_in['b1'], 'L0_gnn_W2': _L0_gnn_in['W2'], 'L0_gnn_att_src2': _L0_gnn_in['att_src2'], 'L0_gnn_att_dst2': _L0_gnn_in['att_dst2'], 'L0_gnn_b2': _L0_gnn_in['b2'], 'L1_gnn_Wq': _L1_gnn_in['Wq'], 'L1_gnn_bq': _L1_gnn_in['bq'], 'L1_gnn_Wk': _L1_gnn_in['Wk'], 'L1_gnn_bk': _L1_gnn_in['bk'], 'L1_gnn_Wv': _L1_gnn_in['Wv'], 'L1_gnn_bv': _L1_gnn_in['bv'], 'L2_gnn_W': _L2_gnn_in['W'], 'L2_gnn_b': _L2_gnn_in['b'], 'L2_gnn_gamma': _L2_gnn_in['gamma'], 'L2_gnn_beta': _L2_gnn_in['beta'], 'L3_gnn_W': _L3_gnn_in['W'], 'L3_gnn_a_self': _L3_gnn_in['a_self'], 'L3_gnn_a_neigh': _L3_gnn_in['a_neigh'], 'L3_gnn_bias': _L3_gnn_in['bias']}

def reference(x, src, dst, edge_attr_64, edge_weight, L0_gnn_W1, L0_gnn_att_src1, L0_gnn_att_dst1, L0_gnn_b1, L0_gnn_W2, L0_gnn_att_src2, L0_gnn_att_dst2, L0_gnn_b2, L1_gnn_Wq, L1_gnn_bq, L1_gnn_Wk, L1_gnn_bk, L1_gnn_Wv, L1_gnn_bv, L2_gnn_W, L2_gnn_b, L2_gnn_gamma, L2_gnn_beta, L3_gnn_W, L3_gnn_a_self, L3_gnn_a_neigh, L3_gnn_bias):
    import jax
    import jax.numpy as jnp

    def _L0_gnn_ref(x, edge_index, W1, att_src1, att_dst1, b1, W2, att_src2, att_dst2, b2):
        import jax, jax.numpy as jnp
        import numpy as np
        N, E = (3125, 50000)
        NFEAT, NHID, NCLASS, HEADS = (256, 256, 64, 4)
        NEG_SLOPE = 0.2

        def gat_conv(x, src, dst, W, a_src, a_dst, b):
            H, C = a_src.shape
            h = (x @ W).reshape(-1, H, C)
            alpha_s = jnp.einsum('nhc,hc->nh', h, a_src)
            alpha_d = jnp.einsum('nhc,hc->nh', h, a_dst)
            e = jax.nn.leaky_relu(alpha_s[src] + alpha_d[dst], NEG_SLOPE)
            m = jax.ops.segment_max(e, dst, num_segments=N)
            ex = jnp.exp(e - m[dst])
            s = jax.ops.segment_sum(ex, dst, num_segments=N)
            alpha = ex / (s[dst] + 1e-16)
            out = jax.ops.segment_sum(h[src] * alpha[:, :, None], dst, num_segments=N)
            return out.reshape(-1, H * C) + b
        loops = jnp.arange(N, dtype=edge_index.dtype)
        src = jnp.concatenate([edge_index[0], loops])
        dst = jnp.concatenate([edge_index[1], loops])
        x0 = jax.nn.relu(gat_conv(x, src, dst, W1, att_src1, att_dst1, b1))
        x2 = gat_conv(x0, src, dst, W2, att_src2, att_dst2, b2)
        return x2

    def _L1_gnn_ref(x, Wq, bq, Wk, bk, Wv, bv, src, dst):
        import jax, jax.numpy as jnp
        import numpy as np
        N_NODES = 3125
        N_EDGES = 50000
        DIM = 256
        HEADS = 8
        DIM_OUT = 32
        n = x.shape[0]
        q = (x @ Wq + bq).reshape(n, HEADS, DIM_OUT)
        k = (x @ Wk + bk).reshape(n, HEADS, DIM_OUT)
        v = (x @ Wv + bv).reshape(n, HEADS, DIM_OUT)
        scores = jnp.einsum('ehd,ehd->eh', q[src], k[dst]) / jnp.sqrt(jnp.asarray(DIM_OUT, dtype=x.dtype))
        m = jax.ops.segment_max(scores, dst, num_segments=n)
        m = jnp.where(jnp.isfinite(m), m, 0.0)
        e = jnp.exp(scores - m[dst])
        z = jax.ops.segment_sum(e, dst, num_segments=n)
        p = e / jnp.maximum(z[dst], 1e-16)
        out = jax.ops.segment_sum(v[src] * p[:, :, None], dst, num_segments=n)
        return out.reshape(n, HEADS * DIM_OUT)

    def _L2_gnn_ref(node_features, edge_index, edge_features, W, b, gamma, beta):
        import jax, jax.numpy as jnp
        import numpy as np
        N_NODES = 25000
        N_EDGES = 18750
        D_NODE = 256
        D_EDGE = 64
        LN_EPS = 0.001
        source = edge_index[0]
        target = edge_index[1]
        msgs = jnp.concatenate([node_features[source], edge_features], axis=-1)
        msgs = jax.nn.silu(msgs @ W + b)
        out = jax.ops.segment_sum(msgs, target, num_segments=node_features.shape[0])
        mean = jnp.mean(out, axis=-1, keepdims=True)
        var = jnp.mean(jnp.square(out - mean), axis=-1, keepdims=True)
        out = (out - mean) * jax.lax.rsqrt(var + LN_EPS) * gamma + beta
        return out

    def _L3_gnn_ref(x, W, a_self, a_neigh, bias, adj_val, edge_row, edge_col):
        import jax, jax.numpy as jnp
        import numpy as np
        N_NODES = 3125
        N_EDGES = 50000
        F_IN = 256
        F_OUT = 64
        HEADS = 4
        LEAKY_ALPHA = 0.2
        N = x.shape[0]
        feats = jnp.einsum('nf,hfo->hno', x, W)
        s_self = jnp.einsum('hno,ho->hn', feats, a_self)
        s_neigh = jnp.einsum('hno,ho->hn', feats, a_neigh)
        z = s_self[:, edge_row] + s_neigh[:, edge_col]
        e = jnp.where(z > 0, z, LEAKY_ALPHA * z) * adj_val[None, :]

        def seg_softmax(e_h):
            m = jax.ops.segment_max(e_h, edge_row, num_segments=N)
            ex = jnp.exp(e_h - m[edge_row])
            s = jax.ops.segment_sum(ex, edge_row, num_segments=N)
            return ex / s[edge_row]
        alpha = jax.vmap(seg_softmax)(e)

        def aggregate(alpha_h, feat_h):
            return jax.ops.segment_sum(alpha_h[:, None] * feat_h[edge_col], edge_row, num_segments=N)
        out = jax.vmap(aggregate)(alpha, feats) + bias[:, None, :]
        out = jnp.transpose(out, (1, 0, 2)).reshape(N, -1)
        return jax.nn.relu(out)
    edge_index = jnp.stack([src, dst])
    h = jnp.maximum(_layernorm(x, axis=-1), 0.0)
    x = x + _L0_gnn_ref(h, edge_index, L0_gnn_W1, L0_gnn_att_src1, L0_gnn_att_dst1, L0_gnn_b1, L0_gnn_W2, L0_gnn_att_src2, L0_gnn_att_dst2, L0_gnn_b2)
    h = jnp.maximum(_layernorm(x, axis=-1), 0.0)
    x = x + _L1_gnn_ref(h, L1_gnn_Wq, L1_gnn_bq, L1_gnn_Wk, L1_gnn_bk, L1_gnn_Wv, L1_gnn_bv, src, dst)
    h = jnp.maximum(_layernorm(x, axis=-1), 0.0)
    x = x + _L2_gnn_ref(h, edge_index, edge_attr_64, L2_gnn_W, L2_gnn_b, L2_gnn_gamma, L2_gnn_beta)
    h = jnp.maximum(_layernorm(x, axis=-1), 0.0)
    x = x + _L3_gnn_ref(h, L3_gnn_W, L3_gnn_a_self, L3_gnn_a_neigh, L3_gnn_bias, edge_weight, src, dst)
    return x

_drawn_inputs = setup_inputs


def setup_inputs(seed=0):
    import zlib

    import numpy as np

    out = dict(_drawn_inputs(seed))
    spreads = {'L0_gnn_b1': (0.0, 0.1),
     'L0_gnn_b2': (0.0, 0.1),
     'L2_gnn_b': (0.0, 0.1),
     'L2_gnn_gamma': (1.0, 0.2),
     'L2_gnn_beta': (0.0, 0.1),
     'L3_gnn_bias': (0.0, 0.1)}
    factors = {'edge_weight': 8.0,
     'L0_gnn_att_dst1': 54.784,
     'L0_gnn_att_src2': 36.567,
     'L0_gnn_att_dst2': 64.0,
     'L1_gnn_Wq': 8.0,
     'L1_gnn_bq': 64.0,
     'L1_gnn_Wk': 8.0,
     'L1_gnn_bk': 8.0,
     'L3_gnn_a_self': 8.0,
     'L3_gnn_a_neigh': 8.0}
    for name, (base, spread) in spreads.items():
        noise = np.random.default_rng([zlib.crc32(name.encode()), seed]).standard_normal(out[name].shape)
        drawn = base * np.exp(spread * noise) if base else spread * noise
        out[name] = jnp.asarray(drawn.astype(out[name].dtype))
    for name, factor in factors.items():
        out[name] = (out[name] * factor).astype(out[name].dtype)
    return out
```

```python
from contextlib import ExitStack

import concourse.bass as bass
from concourse import mybir

P = 128
ALU = mybir.AluOpType
ACT = mybir.ActivationFunctionType
F32 = mybir.dt.float32
BF16 = mybir.dt.bfloat16
I32 = mybir.dt.int32
U32 = mybir.dt.uint32
AX = mybir.AxisListType
ENG = mybir.EngineType

N, D, E, DE = 3125, 256, 100000, 64
NB = -(-N // P)
NP = NB * P
GX = NB + 1
STEP = 16
HALF = 8
QUAD = 4
T = -(-(E // P + 1) // STEP) * STEP
EP = T * P
U = -(-(T + NB - 1) // STEP) * STEP
UC = -(-U // P)
UP = UC * P
TR = T // UC
TURNS = U // STEP
PADNODE = NP - 1
ACCW = D + 8
BIG = 1e30
LN_EPS = 1e-5
assert T % UC == 0 and TR <= P and E % P == 32


class Steps:

    def __init__(self, sem):
        self.sem, self.n = sem, 0

    def up(self, instruction, by=1):
        instruction.then_inc(self.sem, by)
        self.n += by

    def own(self, eng, instruction):
        self.up(instruction)
        eng.wait_ge(self.sem, self.n)


def gnn_kernel(nc, x_in, src_in, dst_in, attr_in, ew_in, W1, as1, ad1, b1, W2, as2, ad2, b2, Wq, bq, Wk, bk, Wv, bv,
               L2W, L2b, L2g, L2be, L3W, L3as, L3an, L3b, out, upto=99, dumps=None):
    ctx = ExitStack()

    def sb(name, shape, dt=F32, c=ctx):
        return c.enter_context(nc.sbuf_tensor(name, shape, dt))

    def ps(name, shape, c, dt=F32):
        return c.enter_context(nc.psum_tensor(name, shape, dt))

    def dram(name, shape, dt=F32):
        return nc.dram_tensor(name, shape, dt, kind="Internal").ap()

    taken = [0]

    class Phase:

        def __init__(self):
            self.sems = []
            taken[0] += 1

        def sem(self, name):
            s = nc.alloc_semaphore(f"{name}_{taken[0]}")
            self.sems.append(s)
            return s

        def end(self):
            nc.clear_and_free_semaphores(self.sems)
            nc.all_engine_barrier()

    def copy(eng, to, of):
        return eng.tensor_scalar(to, of, 1.0, None, ALU.mult)

    def flat(ap):
        return ap.rearrange("(a b) -> a b", a=1)

    ident = sb("ident", [P, P])
    iota_row = sb("iota_row", [P, P])
    iota_col = sb("iota_col", [P, 1])
    earlier = sb("earlier", [P, P])
    later = sb("later", [P, P])
    ones = sb("ones", [P, P])
    eps = sb("eps", [P, 1])
    unit_of = sb("unit_of", [4, UP], I32)
    order = {}
    for o, gt in (("d", 0), ("s", 2)):
        order[o] = {
            "rel": sb(f"rel_{o}", [P, UP]),
            "oth": sb(f"oth_{o}", [P, UP], U32),
            "ohi": sb(f"ohi_{o}", [P, UP]),
            "gof": unit_of[gt:gt + 1, :],
            "tof": unit_of[gt + 1:gt + 2, :],
            "relrow": dram(f"relrow_{o}", [UP, P], BF16),
            "lorow": dram(f"lorow_{o}", [UP, P], BF16),
            "keyrow": dram(f"keyrow_{o}", [UP, P]),
            "wrow": dram(f"wrow_{o}", [UP, P]),
            "recs": dram(f"recs_{o}", [EP, 4]),
        }
    attr_pad = dram("attr_pad", [EP, DE])
    tab_a = dram("tab_a", [NP, D])
    tab_b = dram("tab_b", [NP, D])
    padded = {k: dram(f"pad_{k}", [T, P], dt) for k, dt in (("src", I32), ("dst", I32), ("w", F32))}
    table_d = dram("table_d", [2, UP], I32)

    def setup():
        ph = Phase()
        consts, chain, stored = (ph.sem(n) for n in ("consts_made", "set_chain", "padded_stored"))
        with ExitStack() as c:
            ii = sb("set_ii", [P, P], I32, c)
            ic = sb("set_ic", [P, 1], I32, c)
            padi = sb("set_padi", [1, EP - E], I32, c)
            zpad = sb("set_zpad", [1, EP - E], F32, c)
            zat = sb("set_zat", [P, DE * (EP - E) // P + DE], F32, c)
            with nc.Block() as block:
                @block.gpsimd
                def _(eng):
                    eng.iota(ii[:, :], [[1, P]], base=0, channel_multiplier=0).then_inc(consts, 1)
                    eng.iota(ic[:, :], [[1, 1]], base=0, channel_multiplier=1).then_inc(consts, 1)

                @block.vector
                def _(eng):
                    st = Steps(chain)
                    st.own(eng, eng.memset(padi[:, :], PADNODE))
                    st.own(eng, eng.memset(zpad[:, :], 0.0))
                    st.own(eng, eng.memset(zat[:, :], 0.0))
                    st.own(eng, eng.memset(ones[:, :], 1.0))
                    st.own(eng, eng.memset(eps[:, :], LN_EPS))
                    eng.wait_ge(consts, 2)
                    st.own(eng, eng.tensor_copy(iota_row[:, :], ii[:, :]))
                    st.own(eng, eng.tensor_copy(iota_col[:, :], ic[:, :]))
                    for tile_, op in ((ident, ALU.is_equal), (earlier, ALU.is_lt), (later, ALU.is_gt)):
                        st.own(eng, eng.tensor_scalar(tile_[:, :], iota_row[:, :], iota_col[:, :], None, op))

                @block.sync
                def _(eng):
                    for key, ap in (("src", src_in), ("dst", dst_in), ("w", ew_in)):
                        eng.dma_start(padded[key].rearrange("t e -> (t e)")[0:E].rearrange("(a b) -> a b", a=32),
                                      ap.rearrange("(a b) -> a b", a=32)).then_inc(stored, 16)
                    eng.wait_ge(chain, 3)
                    for key, tile_ in (("src", padi), ("dst", padi), ("w", zpad)):
                        eng.dma_start(flat(padded[key].rearrange("t e -> (t e)")[E:EP]), tile_[:, :])\
                            .then_inc(stored, 16)
                    eng.dma_start(attr_pad[E:E + P * 2, :].rearrange("(p k) d -> p (k d)", p=P), zat[:, 0:2 * DE])\
                        .then_inc(stored, 16)
                    rest = EP - E - 2 * P
                    if rest > 0:
                        full_, left = rest // P, rest % P
                        for k in range(full_):
                            a0 = E + (2 + k) * P
                            eng.dma_start(attr_pad[a0:a0 + P, :], zat[:, 0:DE]).then_inc(stored, 16)
                        a0 = EP - left
                        if left:
                            eng.dma_start(attr_pad[a0:EP, :], zat[0:left, 0:DE]).then_inc(stored, 16)
                    n_more = full_ + (1 if left else 0)
                    eng.wait_ge(stored, 16 * (7 + n_more + 1))

                @block.scalar
                def _(eng):
                    eng.dma_start(attr_pad[0:E, :].rearrange("(a b) d -> a (b d)", a=16),
                                  attr_in.rearrange("(a b) d -> a (b d)", a=16)).then_inc(stored, 16)
        ph.end()

    def transpose_block(eng, out_ps, in_sb):
        return eng.transpose(out_ps, in_sb, ident[0:in_sb.shape[0], 0:in_sb.shape[0]])

    def records():
        ph = Phase()
        loaded, built, stored = (ph.sem(n) for n in ("rows_loaded", "recs_built", "recs_stored"))
        with ExitStack() as c:
            raw = {k: sb(f"raw_{k}", [TR, UC, P], dt, c) for k, dt in (("src", I32), ("dst", I32), ("w", F32))}
            rec = sb("rec_rows", [TR, UC, P, 4], F32, c)
            with nc.Block() as block:
                @block.sync
                def _(eng):
                    for k in raw:
                        eng.dma_start(raw[k][:, :, :], padded[k].rearrange("(c p) e -> p c e", p=TR))\
                            .then_inc(loaded, 16)
                    eng.wait_ge(built, 4)
                    eng.dma_start(order["d"]["recs"].rearrange("(c p e) f -> p c (e f)", p=TR, e=P),
                                  rec[:, :, :, :].rearrange("p c e f -> p c (e f)")).then_inc(stored, 16)
                    eng.wait_ge(stored, 16)

                @block.vector
                def _(eng):
                    eng.wait_ge(loaded, 48)
                    eng.tensor_copy(rec[:, :, :, 0], raw["dst"][:, :, :]).then_inc(built, 1)
                    eng.tensor_copy(rec[:, :, :, 1], raw["src"][:, :, :]).then_inc(built, 1)
                    eng.tensor_copy(rec[:, :, :, 2], raw["w"][:, :, :]).then_inc(built, 1)
                    eng.memset(rec[:, :, :, 3], 0.0).then_inc(built, 1)
        ph.end()

    def sort_by_source():
        with ExitStack() as c:
            key_e = sb("key_e", [P, T], F32, c)
            lo_e = sb("lo_e", [P, T], F32, c)
            hi_e = sb("hi_e", [P, T], F32, c)
            rec_e = sb("rec_e", [P, T, 4], F32, c)
            start = sb("start", [P, NB], F32, c)
            lorow_f = dram("lorow_f", [T, P])
            keyrow_f = dram("keyrow_f", [T, P])

            ph = Phase()
            rows, made, turned, copied, saved = (ph.sem(n) for n in ("srt_rows", "srt_made", "srt_turned", "srt_copied", "srt_saved"))
            with ExitStack() as c2:
                rec = sb("srt_rec", [TR, UC, P, 4], F32, c2)
                ki = sb("srt_ki", [TR, UC, P], I32, c2)
                lo_i = sb("srt_lo_i", [TR, UC, P], I32, c2)
                hi_i = sb("srt_hi_i", [TR, UC, P], I32, c2)
                planes = sb("srt_planes", [TR, 5, UC, P], F32, c2)
                pt = ps("srt_pt", [P, 4, 512], c2)
                dests = [rec_e[:, :, 0], rec_e[:, :, 1], rec_e[:, :, 2], lo_e[:, :], hi_e[:, :]]
                with nc.Block() as block:
                    @block.sync
                    def _(eng):
                        eng.dma_start(rec[:, :, :, :].rearrange("p c e f -> p c (e f)"),
                                      order["d"]["recs"].rearrange("(c p e) f -> p c (e f)", p=TR, e=P))\
                            .then_inc(rows, 16)
                        eng.wait_ge(made, 8)
                        eng.dma_start(lorow_f.rearrange("(c p) e -> p c e", p=TR), planes[:, 3, :, :])\
                            .then_inc(saved, 16)
                        eng.dma_start(keyrow_f.rearrange("(c p) e -> p c e", p=TR), planes[:, 0, :, :])\
                            .then_inc(saved, 16)
                        eng.wait_ge(saved, 32)

                    @block.vector
                    def _(eng):
                        st = Steps(made)
                        eng.wait_ge(rows, 16)
                        st.own(eng, eng.tensor_copy(planes[:, 0, :, :], rec[:, :, :, 1]))
                        st.own(eng, eng.tensor_copy(planes[:, 1, :, :], rec[:, :, :, 0]))
                        st.own(eng, eng.tensor_copy(planes[:, 2, :, :], rec[:, :, :, 2]))
                        st.own(eng, eng.tensor_copy(ki[:, :, :], rec[:, :, :, 1]))
                        st.own(eng, eng.tensor_scalar(lo_i[:, :, :], ki[:, :, :], P - 1, None, ALU.bitwise_and))
                        st.own(eng, eng.tensor_scalar(hi_i[:, :, :], ki[:, :, :], 7, None, ALU.logical_shift_right))
                        st.own(eng, eng.tensor_copy(planes[:, 3, :, :], lo_i[:, :, :]))
                        st.own(eng, eng.tensor_copy(planes[:, 4, :, :], hi_i[:, :, :]))
                        st.own(eng, eng.memset(rec_e[:, :, 3], 0.0))
                        for k in range(5 * UC):
                            pl, ch = divmod(k, UC)
                            eng.wait_ge(turned, k + 1)
                            eng.tensor_copy(dests[pl][:, ch * TR:(ch + 1) * TR], pt[:, k % 4, 0:TR]).then_inc(copied, 1)
                        eng.wait_ge(copied, 5 * UC)
                        eng.tensor_copy(key_e[:, :], rec_e[:, :, 0]).then_inc(copied, 1)

                    @block.tensor
                    def _(eng):
                        eng.wait_ge(made, 8)
                        for k in range(5 * UC):
                            pl, ch = divmod(k, UC)
                            if k >= 4:
                                eng.wait_ge(copied, k - 3)
                            transpose_block(eng, pt[:, k % 4, 0:TR], planes[:, pl, ch, :]).then_inc(turned, 1)
            ph.end()

            ph = Phase()
            hot, summed, placed = (ph.sem(n) for n in ("hst_hot", "hst_summed", "hst_placed"))
            with ExitStack() as c2:
                ohl = sb("hst_lo", [P, STEP, P], BF16, c2)
                ohh = sb("hst_hi", [P, STEP, NB], BF16, c2)
                zero = sb("hst_zero", [P, P], BF16, c2)
                counts = sb("hst_counts", [P, NB], F32, c2)
                run = sb("hst_run", [P, NB], F32, c2)
                hist = ps("hst_ps", [P, NB], c2)
                below = ps("hst_below", [P, 2, NB], c2)
                with nc.Block() as block:
                    @block.vector
                    def _(eng):
                        eng.memset(zero[:, :], 0.0).then_inc(hot, 2)
                        with eng.Fori(0, T // STEP) as i:
                            for h in range(2):
                                hs, ts = slice(h * HALF, (h + 1) * HALF), bass.ds(i * STEP + h * HALF, HALF)
                                eng.wait_ge(summed, i * STEP + HALF * (h + 1))
                                for oh, digit, width in ((ohl, lo_e, P), (ohh, hi_e, NB)):
                                    eng.tensor_tensor(
                                        oh[:, hs, :],
                                        iota_row[:, 0:width].rearrange("p (o n) -> p o n", o=1).to_broadcast([P, HALF, width]),
                                        digit[:, ts].rearrange("p (u o) -> p u o", o=1).to_broadcast([P, HALF, width]),
                                        ALU.is_equal).then_inc(hot, 1)
                        st = Steps(placed)
                        eng.wait_ge(summed, T + STEP + 1)
                        st.own(eng, eng.tensor_copy(counts[:, :], hist[:, :]))
                        eng.wait_ge(summed, T + STEP + 3)
                        st.own(eng, eng.tensor_tensor_scan(run[:, :], ones[:, 0:NB], below[:, 1, :], 0.0, ALU.mult, ALU.add))
                        st.own(eng, eng.tensor_tensor(run[:, :], run[:, :], below[:, 1, :], ALU.subtract))
                        st.own(eng, eng.tensor_tensor(start[:, :], run[:, :], below[:, 0, :], ALU.add))

                    @block.tensor
                    def _(eng):
                        eng.sem_inc(summed, STEP)
                        eng.wait_ge(hot, 2)
                        eng.matmul(hist[:, :], zero[:, :], zero[:, 0:NB], start=True, stop=False, skip_group_check=True)
                        with eng.Fori(0, T // STEP) as i:
                            for k in range(STEP):
                                if k % HALF == 0:
                                    eng.wait_ge(hot, i * 4 + 2 * (k // HALF) + 4)
                                eng.matmul(hist[:, :], ohl[:, k, :], ohh[:, k, :], start=False, stop=False,
                                           skip_group_check=True).then_inc(summed, 1)
                        eng.matmul(hist[:, :], zero[:, :], zero[:, 0:NB], start=False, stop=True,
                                   skip_group_check=True).then_inc(summed, 1)
                        eng.wait_ge(placed, 1)
                        eng.matmul(below[:, 0, :], later[:, :], counts[:, :], start=True, stop=True).then_inc(summed, 1)
                        eng.matmul(below[:, 1, :], ones[:, :], counts[:, :], start=True, stop=True).then_inc(summed, 1)
            ph.end()

            ph = Phase()
            rowin = [ph.sem(f"plc_rows{h}") for h in range(2)]
            hot, count_done, base_ready, picked, posted, sent = (
                ph.sem(n) for n in ("plc_hot", "plc_counted", "plc_base", "plc_picked", "plc_posted", "plc_fed"))
            seen = ph.sem("plc_seen")
            landed = [ph.sem(f"plc_landed{k}") for k in range(STEP)]
            with ExitStack() as c2:
                krow = sb("plc_krow", [P, 2, HALF * P], F32, c2)
                lrow = sb("plc_lrow", [P, 2, HALF * P], F32, c2)
                lot = sb("plc_lot", [P, 2, HALF * P], F32, c2)
                ohl = sb("plc_ohl", [P, STEP, P], BF16, c2)
                ohh = sb("plc_ohh", [P, STEP, NB], BF16, c2)
                base = sb("plc_base_sb", [P, 2, NB], F32, c2)
                junk = sb("plc_junk", [P, HALF, P], F32, c2)
                junk2 = sb("plc_junk2", [P, HALF, NB], F32, c2)
                rank = sb("plc_rank", [P, STEP], F32, c2)
                before = sb("plc_before", [P, STEP], F32, c2)
                posu = sb("plc_posu", [P, STEP], U32, c2)
                recr = sb("plc_recr", [P, STEP, 4], F32, c2)
                hist = ps("plc_hist", [P, NB], c2)
                got = ps("plc_got", [P, 2, 512], c2)
                LOOPV = 2 * (1 + 4 * HALF + 3)
                TT = T // STEP
                with nc.Block() as block:
                    @block.sync
                    def _(eng):
                        with eng.Fori(0, TT) as i:
                            for h in range(2):
                                eng.wait_ge(hot, i * LOOPV + (LOOPV // 2) * (h + 1))
                                for rowbuf, rows_d in ((krow, keyrow_f), (lrow, lorow_f)):
                                    eng.dma_start(
                                        rowbuf[:, h, :],
                                        rows_d[bass.ds(i * STEP + h * HALF, HALF), :].rearrange("(o t) e -> o (t e)", o=1)
                                        .to_broadcast([P, HALF * P])).then_inc(rowin[h], 16)

                    @block.vector
                    def _(eng):
                        eng.sem_inc(hot, LOOPV)
                        with eng.Fori(0, TT) as i:
                            n = [0]

                            def own(ins, wait=False):
                                ins.then_inc(hot, 1)
                                n[0] += 1
                                if wait:
                                    eng.wait_ge(hot, i * LOOPV + (LOOPV + n[0]))

                            for h in range(2):
                                eng.wait_ge(rowin[h], i * 32 + 32)
                                own(eng.tensor_scalar(lot[:, h, :], lrow[:, h, :], iota_col[:, :], None, ALU.is_equal))
                                for k in range(h * HALF, (h + 1) * HALF + 1):
                                    if k < (h + 1) * HALF:
                                        t = bass.ds(i * STEP + k, 1)
                                        own(eng.tensor_scalar(ohl[:, k, :], iota_row[:, :], lo_e[:, t], None, ALU.is_equal))
                                        own(eng.tensor_scalar(ohh[:, k, :], iota_row[:, 0:NB], hi_e[:, t], None, ALU.is_equal))
                                        own(eng.scalar_tensor_tensor(
                                            out=junk[:, k % HALF, :], in0=krow[:, h, (k - h * HALF) * P:(k - h * HALF + 1) * P],
                                            scalar=key_e[:, t], in1=earlier[:, :], op0=ALU.is_equal, op1=ALU.mult,
                                            accum_out=rank[:, k:k + 1]))
                                    if k > h * HALF:
                                        eng.wait_ge(picked, i * STEP + k)
                                        own(eng.scalar_tensor_tensor(
                                            out=junk2[:, (k - 1) % HALF, :], in0=got[:, (k - 1) % 2, 0:NB], scalar=1.0,
                                            in1=ohh[:, k - 1, :], op0=ALU.mult, op1=ALU.mult,
                                            accum_out=before[:, k - 1:k]), wait=(k == (h + 1) * HALF))
                                hs = slice(h * HALF, (h + 1) * HALF)
                                own(eng.tensor_tensor(rank[:, hs], rank[:, hs], before[:, hs], ALU.add), wait=True)
                                eng.wait_ge(sent, i * 2 + h + 1)
                                own(eng.tensor_copy(posu[:, hs], rank[:, hs]))
                                own(eng.tensor_copy(recr[:, hs, :], rec_e[:, bass.ds(i * STEP + h * HALF, HALF), :]))

                    @block.tensor
                    def _(eng):
                        eng.matmul(hist[:, :], ident[:, :], start[:, :], start=True, stop=False,
                                   skip_group_check=True).then_inc(count_done, 1)
                        with eng.Fori(0, TT) as i:
                            for k in range(STEP):
                                h = k // HALF
                                kk = k - h * HALF
                                eng.wait_ge(hot, i * LOOPV + (LOOPV + h * (LOOPV // 2) + max(3, 4 * kk + 2)))
                                eng.wait_ge(base_ready, i * STEP + k + 1)
                                eng.matmul(got[:, k % 2, 0:NB], lot[:, h, kk * P:(kk + 1) * P], base[:, k % 2, :],
                                           start=True, stop=True).then_inc(picked, 1)
                                eng.matmul(hist[:, :], ohl[:, k, :], ohh[:, k, :], start=False, stop=False,
                                           skip_group_check=True).then_inc(count_done, 1)

                    @block.scalar
                    def _(eng):
                        with eng.Fori(0, TT) as i:
                            for k in range(STEP):
                                eng.wait_ge(count_done, i * STEP + k + 1)
                                eng.activation(base[:, k % 2, :], hist[:, :], ACT.Copy).then_inc(base_ready, 1)

                    @block.gpsimd
                    def _(eng):
                        eng.sem_inc(sent, 2)

                        def scatter(i, h):
                            eng.wait_ge(hot, i * LOOPV + (LOOPV + (LOOPV // 2) * (h + 1)))
                            eng.sem_inc(seen, 1)
                            for k in range(h * HALF, (h + 1) * HALF):
                                eng.indirect_dma_start(
                                    out=order["s"]["recs"],
                                    out_offset=bass.IndirectOffsetOnAxis(ap=posu[:, k:k + 1], axis=0),
                                    in_=recr[:, k, :], in_offset=None).then_inc(landed[k], 16)

                        def release(i, h):
                            for k in range(h * HALF, (h + 1) * HALF):
                                eng.wait_ge(landed[k], i * 16 + 16)
                            eng.sem_inc(sent, 1)

                        scatter(0, 0)
                        scatter(0, 1)
                        release(0, 0)
                        with eng.Fori(0, TT - 1) as i:
                            scatter(i + 1, 0)
                            release(i, 1)
                            scatter(i + 1, 1)
                            release(i + 1, 0)
                        release(TT - 1, 1)
            ph.end()

    def units(o):
        od = order[o]
        with ExitStack() as c:
            ucol_i = sb(f"un_ui_{o}", [P, UC], I32, c)
            tio_i = sb(f"un_ti_{o}", [P, T], I32, c)
            ucol = sb(f"un_u_{o}", [P, UC], F32, c)
            tio = sb(f"un_t_{o}", [P, T], F32, c)
            ends = sb(f"un_ends_{o}", [1, 2, T], F32, c)
            endi = sb(f"un_endi_{o}", [1, 2, T], I32, c)
            uv = sb(f"un_uv_{o}", [1, 2, T], F32, c)
            cnt = sb(f"un_cnt_{o}", [1, T], F32, c)
            uvb = sb(f"un_uvb_{o}", [P, 2, T], F32, c)
            junk = sb(f"un_junk_{o}", [P, T], F32, c)
            tu = sb(f"un_tu_{o}", [P, UC], F32, c)
            gu = sb(f"un_gu_{o}", [P, UC], F32, c)
            g128 = sb(f"un_g128_{o}", [P, UC], F32, c)
            tuu = sb(f"un_tuu_{o}", [P, UC], U32, c)
            tgi = sb(f"un_tgi_{o}", [P, 2, UC], I32, c)
            rec = sb(f"un_rec_{o}", [P, UC, P, 4], F32, c)
            rel = sb(f"un_rel_{o}", [P, UC, P], F32, c)
            othi = sb(f"un_othi_{o}", [P, UC, P], I32, c)
            bits = sb(f"un_bits_{o}", [P, UC, P], I32, c)
            hi = sb(f"un_hi_{o}", [P, UC, P], F32, c)
            oth = sb(f"un_oth_{o}", [P, UC, P], F32, c)
            lob = sb(f"un_lob_{o}", [P, UC, P], BF16, c)
            relb = sb(f"un_relb_{o}", [P, UC, P], BF16, c)
            ok = sb(f"un_ok_{o}", [P, UC, P], F32, c)
            keym = sb(f"un_key_{o}", [P, UC, P], F32, c)
            wrow = sb(f"un_w_{o}", [P, UC, P], F32, c)
            pb = ps(f"un_pb_{o}", [P, 2, 2, 512], c)
            pt = ps(f"un_pt_{o}", [P, 4, 512], c)
            ph = Phase()
            loaded, iotas, chain, mm, gathered, saved, turned, copied = (
                ph.sem(n) for n in ("un_loaded", "un_iotas", "un_chain", "un_bcast", "un_gathered", "un_saved", "un_turned", "un_copied"))
            HT = T // 2
            marks = {}
            with nc.Block() as block:
                @block.vector
                def _(eng):
                    st = Steps(chain)

                    def own(ins):
                        st.own(eng, ins)

                    eng.wait_ge(iotas, 2)
                    own(eng.tensor_copy(ucol[:, :], ucol_i[:, :]))
                    own(eng.tensor_copy(tio[:, :], tio_i[:, :]))
                    eng.wait_ge(loaded, 32)
                    own(eng.tensor_copy(endi[:, :, :], ends[:, :, :]))
                    own(eng.tensor_scalar(endi[:, :, :], endi[:, :, :], 7, None, ALU.logical_shift_right))
                    own(eng.tensor_copy(ends[:, :, :], endi[:, :, :]))
                    own(eng.scalar_tensor_tensor(out=cnt[:, :], in0=ends[:, 1, :], scalar=1.0, in1=ends[:, 0, :],
                                                 op0=ALU.add, op1=ALU.subtract))
                    own(eng.tensor_tensor_scan(uv[:, 0, :], ones[0:1, 0:1].to_broadcast([1, T]), cnt[:, :], 0.0,
                                               ALU.mult, ALU.add))
                    own(eng.tensor_tensor(uv[:, 0, :], uv[:, 0, :], cnt[:, :], ALU.subtract))
                    own(eng.tensor_tensor(uv[:, 1, :], ends[:, 0, :], uv[:, 0, :], ALU.subtract))
                    marks["uv"] = st.n
                    eng.wait_ge(mm, 4)
                    for a in range(2):
                        own(eng.tensor_copy(uvb[:, a, :].rearrange("p (h t) -> p h t", h=2), pb[:, a, :, 0:HT]))
                    for j in range(UC):
                        own(eng.tensor_scalar(junk[:, :], uvb[:, 0, :], ucol[:, j:j + 1], None, ALU.is_le, ALU.add,
                                              accum_out=tu[:, j:j + 1]))
                    own(eng.tensor_scalar(tu[:, :], tu[:, :], -1.0, None, ALU.add))
                    own(eng.tensor_copy(tuu[:, :], tu[:, :]))
                    marks["tuu"] = st.n
                    for j in range(UC):
                        own(eng.scalar_tensor_tensor(out=junk[:, :], in0=tio[:, :], scalar=tu[:, j:j + 1],
                                                     in1=uvb[:, 1, :], op0=ALU.is_equal, op1=ALU.mult,
                                                     accum_out=gu[:, j:j + 1]))
                    own(eng.tensor_tensor(gu[:, :], gu[:, :], ucol[:, :], ALU.add))
                    own(eng.tensor_scalar(gu[:, :], gu[:, :], float(NB), None, ALU.min))
                    own(eng.tensor_copy(tgi[:, 0, :], tu[:, :]))
                    own(eng.tensor_copy(tgi[:, 1, :], gu[:, :]))
                    marks["tgi"] = st.n
                    own(eng.tensor_scalar(g128[:, :], gu[:, :], float(P), None, ALU.mult))
                    for j in range(UC):
                        eng.wait_ge(gathered, 16 * (j + 1))
                        own(eng.tensor_scalar(rel[:, j, :], rec[:, j, :, 0], g128[:, j:j + 1], None, ALU.subtract))
                    own(eng.tensor_copy(wrow[:, :, :], rec[:, :, :, 2]))
                    own(eng.tensor_copy(oth[:, :, :], rec[:, :, :, 1]))
                    own(eng.tensor_copy(othi[:, :, :], oth[:, :, :]))
                    own(eng.tensor_scalar(bits[:, :, :], othi[:, :, :], P - 1, None, ALU.bitwise_and))
                    own(eng.tensor_copy(lob[:, :, :], bits[:, :, :]))
                    own(eng.tensor_scalar(bits[:, :, :], othi[:, :, :], 7, None, ALU.logical_shift_right))
                    own(eng.tensor_copy(hi[:, :, :], bits[:, :, :]))
                    own(eng.tensor_copy(relb[:, :, :], rel[:, :, :]))
                    own(eng.tensor_scalar(ok[:, :, :], rel[:, :, :], 0.0, None, ALU.is_ge))
                    own(eng.scalar_tensor_tensor(out=ok[:, :, :], in0=rel[:, :, :], scalar=float(P), in1=ok[:, :, :],
                                                 op0=ALU.is_lt, op1=ALU.mult))
                    own(eng.scalar_tensor_tensor(out=keym[:, :, :], in0=rec[:, :, :, 0], scalar=1.0, in1=ok[:, :, :],
                                                 op0=ALU.add, op1=ALU.mult))
                    own(eng.tensor_scalar(keym[:, :, :], keym[:, :, :], -1.0, None, ALU.add))
                    marks["rows"] = st.n
                    for k in range(3 * UC):
                        which, j = divmod(k, UC)
                        dest = (od["rel"], od["oth"], od["ohi"])[which]
                        eng.wait_ge(turned, k + 1)
                        eng.tensor_copy(dest[:, j * P:(j + 1) * P], pt[:, k % 4, 0:P]).then_inc(copied, 1)
                    eng.wait_ge(copied, 3 * UC)

                @block.gpsimd
                def _(eng):
                    eng.iota(ucol_i[:, :], [[P, UC]], base=0, channel_multiplier=1).then_inc(iotas, 1)
                    eng.iota(tio_i[:, :], [[1, T]], base=0, channel_multiplier=0).then_inc(iotas, 1)
                    eng.wait_ge(chain, marks["tuu"])
                    for j in range(UC):
                        eng.indirect_dma_start(out=rec[:, j, :, :].rearrange("p e f -> p (e f)"), out_offset=None,
                                               in_=od["recs"].rearrange("(t e) f -> t (e f)", e=P),
                                               in_offset=bass.IndirectOffsetOnAxis(ap=tuu[:, j:j + 1], axis=0))\
                            .then_inc(gathered, 16)
                        eng.wait_ge(gathered, 16 * (j + 1))

                @block.sync
                def _(eng):
                    keys = od["recs"].rearrange("(t e) f -> t e f", e=P)
                    with nc.allow_non_contiguous_dma(reason="first and last keys of the tiles"):
                        eng.dma_start(ends[:, 0, :], keys[:, 0, 0:1].rearrange("t o -> o t")).then_inc(loaded, 16)
                        eng.dma_start(ends[:, 1, :], keys[:, P - 1, 0:1].rearrange("t o -> o t")).then_inc(loaded, 16)
                    eng.wait_ge(chain, marks["tgi"])
                    with nc.allow_non_contiguous_dma(reason="tables of units"):
                        for a in range(2):
                            eng.dma_start(table_d[a, :].rearrange("(c p) -> p c", p=P), tgi[:, a, :]).then_inc(saved, 16)
                    eng.wait_ge(saved, 32)
                    eng.dma_start(od["tof"], table_d[0:1, :]).then_inc(saved, 16)
                    eng.dma_start(od["gof"], table_d[1:2, :]).then_inc(saved, 16)
                    eng.wait_ge(chain, marks["rows"])
                    for name, tile_ in (("relrow", relb), ("lorow", lob), ("keyrow", keym), ("wrow", wrow)):
                        eng.dma_start(od[name].rearrange("(c p) e -> p c e", p=P), tile_[:, :, :]).then_inc(saved, 16)
                    eng.wait_ge(saved, 32 + 32 + 64)

                @block.tensor
                def _(eng):
                    eng.wait_ge(chain, marks["uv"])
                    for a in range(2):
                        for h in range(2):
                            eng.matmul(pb[:, a, h, 0:HT], ones[0:1, :], uv[:, a, h * HT:(h + 1) * HT],
                                       start=True, stop=True).then_inc(mm, 1)
                    eng.wait_ge(chain, marks["rows"])
                    for k in range(3 * UC):
                        which, j = divmod(k, UC)
                        if k >= 4:
                            eng.wait_ge(copied, k - 3)
                        transpose_block(eng, pt[:, k % 4, 0:P], (rel, oth, hi)[which][:, j, :]).then_inc(turned, 1)
            ph.end()

    def dense(tag, given, norm, mats, w_ap=None, b_aps=(), scores=None, k_split=None, stores=()):
        M = len(mats)
        with ExitStack() as c:
            W = sb(f"dn_w_{tag}", [P, 2, M * D], F32, c)
            B = sb(f"dn_b_{tag}", [P, max(1, len(b_aps)), D], F32, c)
            V = sb(f"dn_v_{tag}", [P, 2, D], F32, c)
            st6 = sb(f"dn_st_{tag}", [P, NB, 6], F32, c)
            mv = sb(f"dn_mv_{tag}", [P, NB, 2], F32, c)
            rstd = sb(f"dn_rstd_{tag}", [P, NB], F32, c)
            hn = sb(f"dn_hn_{tag}", [P, 2, D], F32, c)
            hT = sb(f"dn_hT_{tag}", [P, 2, 2, P], F32, c)
            prod = sb(f"dn_prod_{tag}", [P, 2, D], F32, c)
            rest = sb(f"dn_rest_{tag}", [P, 3, D], F32, c)
            pT = ps(f"dn_pT_{tag}", [P, 2, 512], c)
            pM = ps(f"dn_pM_{tag}", [P, 3, 512], c)
            ph = Phase()
            wl, stat, std, normed, scaled, turned, relued, done, outed, saved = (
                ph.sem(n) for n in ("dn_weights", "dn_stats", "dn_std", "dn_normed", "dn_scaled", "dn_turned", "dn_relued", "dn_summed", "dn_out", "dn_saved"))
            n_w = len(w_ap) + len(b_aps) + (2 if scores else 0)
            per = M + (5 if k_split else 0) + (4 if scores else 0)
            with nc.Block() as block:
                @block.sync
                def _(eng):
                    for dst, src in w_ap:
                        eng.dma_start(dst(W), src).then_inc(wl, 16)
                    for j, b in enumerate(b_aps):
                        eng.dma_start(B[:, j, :], flat(b).to_broadcast([P, D])).then_inc(wl, 16)
                    if scores:
                        for j, v in enumerate(scores):
                            eng.dma_start(V[:, j, :], v.rearrange("(o h) f -> o (h f)", o=1).to_broadcast([P, D]))\
                                .then_inc(wl, 16)
                    if stores:
                        eng.wait_ge(outed, per * NB + per)
                    for tile_, table in stores:
                        eng.dma_start(table.rearrange("(b p) d -> p b d", p=P), tile_[:, :, :]).then_inc(saved, 16)
                    if stores:
                        eng.wait_ge(saved, 16 * len(stores))

                @block.scalar
                def _(eng):
                    if norm:
                        eng.wait_ge(stat, NB + 1)
                        eng.activation(rstd[:, :], mv[:, :, 1], ACT.Sqrt, bias=eps[:, :]).then_inc(std, 1)
                    with eng.Fori(0, NB) as i:
                        eng.wait_ge(turned, i + 1)
                        eng.activation(hT[:, 0, :, :], pT[:, 0, 0:D].rearrange("p (k n) -> p k n", k=2), ACT.Relu)\
                            .then_inc(relued, 1)

                @block.tensor
                def _(eng):
                    eng.wait_ge(wl, 16 * n_w)
                    with eng.Fori(0, NB) as i:
                        eng.wait_ge(scaled, i + 1)
                        for k in range(2):
                            tr = eng.transpose(pT[:, 0, k * P:(k + 1) * P], hn[:, 0, k * P:(k + 1) * P], ident[:, :])
                        tr.then_inc(turned, 1)
                        eng.wait_ge(relued, i + 1)
                        eng.wait_ge(outed, i * per + M)
                        for m in range(M):
                            for k in range(2):
                                mm = eng.matmul(pM[:, m, 0:D], hT[:, 0, k, :], W[:, k, m * D:(m + 1) * D],
                                                start=(k == 0), stop=(k == 1))
                        mm.then_inc(done, 1)

                @block.vector
                def _(eng):
                    eng.wait_ge(wl, 16 * n_w)
                    if norm:
                        for b in range(NB):
                            eng.bn_stats(st6[:, b, :], given[:, b, :]).then_inc(normed, 1)
                            eng.wait_ge(normed, b + 1)
                            eng.bn_aggr(mv[:, b, :], st6[:, b, :]).then_inc(stat, 1)
                        eng.engine_nop().then_inc(stat, 1)
                        eng.wait_ge(stat, NB + 1)
                        eng.wait_ge(std, 1)
                        eng.reciprocal(rstd[:, :], rstd[:, :]).then_inc(std, 1)
                        eng.wait_ge(std, 2)
                    if k_split:
                        eng.memset(k_split[:, NB, :, :], 0.0).then_inc(outed, 1)
                        eng.wait_ge(outed, 1)
                    eng.sem_inc(outed, per - (1 if k_split else 0))

                    def scale(i):
                        bi = bass.ds(i, 1)
                        if norm:
                            ins = eng.tensor_scalar(hn[:, 0:1, :], given[:, bi, :], mv[:, bi, 0:1].rearrange("p a b -> p (a b)"),
                                                    rstd[:, bi], ALU.subtract, ALU.mult)
                        else:
                            ins = copy(eng, hn[:, 0:1, :], given[:, bi, :])
                        ins.then_inc(scaled, 1)

                    def finish_block(i, more):
                        n = [0]

                        def own(ins, wait=True):
                            ins.then_inc(outed, 1)
                            n[0] += 1
                            if wait:
                                eng.wait_ge(outed, i * per + (per + n[0]))

                        bi = bass.ds(i, 1)
                        if more:
                            eng.wait_ge(turned, i + 1)
                            scale(i + 1)
                        eng.wait_ge(done, i + 1)
                        for m, dest in enumerate(mats):
                            if dest is not None and b_aps:
                                own(eng.tensor_tensor(dest[:, bi, :], pM[:, m:m + 1, 0:D], B[:, m:m + 1, :], ALU.add),
                                    wait=False)
                            elif dest is not None:
                                own(copy(eng, dest[:, bi, :], pM[:, m:m + 1, 0:D]), wait=bool(scores))
                        for m, dest in enumerate(mats):
                            if dest is None:
                                own(eng.tensor_tensor(rest[:, 0, :], pM[:, m, 0:D], B[:, m, :], ALU.add))
                                ks = lambda part: k_split[:, bi, part, :].rearrange("p o n -> p (o n)")
                                own(copy(eng, ks(0), rest[:, 0, :]))
                                own(eng.tensor_tensor(rest[:, 1, :], rest[:, 0, :], ks(0), ALU.subtract))
                                own(copy(eng, ks(1), rest[:, 1, :]))
                                own(eng.tensor_tensor(rest[:, 2, :], rest[:, 1, :], ks(1), ALU.subtract))
                                own(copy(eng, ks(2), rest[:, 2, :]))
                        if scores:
                            for j in range(2):
                                own(eng.tensor_tensor(prod[:, j:j + 1, :], mats[0][:, bi, :], V[:, j:j + 1, :], ALU.mult),
                                    wait=(j == 1))
                            for j in range(2):
                                own(eng.tensor_reduce(score_own[:, bi, 4 * j:4 * j + 4],
                                                      prod[:, j:j + 1, :].rearrange("p o (h f) -> p o h f", h=4), AX.X,
                                                      ALU.add), wait=(j == 1))

                    scale(0)
                    with eng.Fori(0, NB - 1) as i:
                        finish_block(i, True)
                    finish_block(NB - 1, False)
            ph.end()

    def score_tables(tag, with_self, gathered_at, own_at):
        ph = Phase()
        chain = ph.sem("tab_chain")
        with ExitStack() as c:
            full = sb(f"tb_full_{tag}", [P, NB, 12], F32, c)
            r1 = sb(f"tb_r1_{tag}", [P, NB, 12], F32, c)
            parts = sb(f"tb_parts_{tag}", [P, 3, NB, 12], BF16, c)
            with nc.Block() as block:
                @block.vector
                def _(eng):
                    st = Steps(chain)
                    own = lambda ins: st.own(eng, ins)
                    g = slice(gathered_at, gathered_at + 4)
                    o = slice(own_at, own_at + 4)
                    own(eng.memset(full[:, :, :], 0.0))
                    own(eng.tensor_copy(full[:, :, 0:4], score_own[:, :, g]))
                    own(eng.tensor_copy(full[:, :, 4:8], score_own[:, :, o]))
                    if with_self:
                        own(eng.tensor_tensor(r1[:, :, 0:4], score_own[:, :, g], score_own[:, :, o], ALU.add))
                        own(eng.scalar_tensor_tensor(out=self_log[:, :, :], in0=r1[:, :, 0:4], scalar=0.2,
                                                     in1=r1[:, :, 0:4], op0=ALU.mult, op1=ALU.max))
                        own(eng.tensor_copy(full[:, :, 8:12], self_log[:, :, :]))
                    own(eng.tensor_copy(parts[:, 0], full[:, :, :]))
                    own(eng.tensor_tensor(r1[:, :, :], full[:, :, :], parts[:, 0], ALU.subtract))
                    own(eng.tensor_copy(parts[:, 1], r1[:, :, :]))
                    own(eng.tensor_tensor(r1[:, :, :], r1[:, :, :], parts[:, 1], ALU.subtract))
                    own(eng.tensor_copy(parts[:, 2], r1[:, :, :]))
                    for part in range(3):
                        own(eng.tensor_copy(a_tab[:, part, :, :], parts[:, part, :, 0:4]))
                        own(eng.tensor_copy(b_tab[:, 0:NB, part, :], parts[:, part, :, 4:12]))
        ph.end()

    def scores_gat(tag, o, with_self):
        od = order[o]
        per = 2 * (6 if with_self else 5)
        BW = 8 if with_self else 4
        with ExitStack() as c:
            rows_o = sb(f"sg_ro_{tag}", [P, 2, HALF * P], BF16, c)
            rows_r = sb(f"sg_rr_{tag}", [P, 2, HALF * P], BF16, c)
            hot_o = sb(f"sg_ho_{tag}", [P, 2, HALF * P], BF16, c)
            hot_r = sb(f"sg_hr_{tag}", [P, 2, HALF * P], BF16, c)
            hot_h = sb(f"sg_hh_{tag}", [P, 2, HALF, NB], F32, c)
            prod = sb(f"sg_pr_{tag}", [P, 2, QUAD, NB, 4], F32, c)
            pick = sb(f"sg_pk_{tag}", [P, 2, HALF, 4], F32, c)
            pa = ps(f"sg_pa_{tag}", [P, 2, 2, 512], c)
            pbk = ps(f"sg_pb_{tag}", [P, 2, 512], c)
            ph = Phase()
            rowin = [ph.sem(f"sg_rows{h}") for h in range(2)]
            vec, fetched, high = ph.sem("sg_vector"), ph.sem("sg_fetched"), ph.sem("sg_high")
            with nc.Block() as block:
                @block.sync
                def _(eng):
                    with eng.Fori(0, TURNS) as i:
                        for h in range(2):
                            eng.wait_ge(vec, i * per + per // 2 * (h + 1))
                            for buf, rows in ((rows_o, od["lorow"]), (rows_r, od["relrow"])):
                                eng.dma_start(buf[:, h, :], rows[bass.ds(i * STEP + h * HALF, HALF), :]
                                              .rearrange("(o t) e -> o (t e)", o=1).to_broadcast([P, HALF * P]))\
                                    .then_inc(rowin[h], 16)

                @block.vector
                def _(eng):
                    def hot_other(h):
                        return eng.tensor_scalar(hot_o[:, h, :], rows_o[:, h, :], iota_col[:, :], None, ALU.is_equal)

                    def hot_own(h):
                        return eng.tensor_scalar(hot_r[:, h, :], rows_r[:, h, :], iota_col[:, :], None, ALU.is_equal)

                    def hot_high(i, h):
                        us = bass.ds(i * STEP + h * HALF, HALF)
                        return eng.tensor_tensor(
                            hot_h[:, h, :, :], iota_row[:, 0:NB].rearrange("p (o n) -> p o n", o=1).to_broadcast([P, HALF, NB]),
                            od["ohi"][:, us].rearrange("p (u o) -> p u o", o=1).to_broadcast([P, HALF, NB]), ALU.is_equal)

                    eng.sem_inc(vec, per)
                    for h in range(2):
                        eng.wait_ge(rowin[h], 32)
                        hot_high(0, h).then_inc(high, 1)
                        hot_other(h).then_inc(vec, per // 2 - 1)
                        hot_own(h).then_inc(vec, 1)

                    def turn(i, more):
                        n = [0]

                        def own(ins, steps=1):
                            ins.then_inc(vec, steps)
                            n[0] += steps

                        for h in range(2):
                            us = bass.ds(i * STEP + h * HALF, HALF)
                            eng.wait_ge(fetched, i * 2 + (h + 1))
                            eng.wait_ge(high, i * 2 + (h + 1))
                            own(eng.tensor_tensor(
                                prod[:, :, :, :, :].rearrange("p a u n h -> p a (u n) h"),
                                pa[:, h, :, 0:QUAD * NB * 4].rearrange("p a (m h) -> p a m h", h=4),
                                hot_h[:, h, :, :].rearrange("p (a u) n -> p a (u n)", a=2)
                                .rearrange("p a (m o) -> p a m o", o=1).to_broadcast([P, 2, QUAD * NB, 4]), ALU.mult))
                            if more:
                                eng.wait_ge(rowin[h], i * 32 + 64)
                                own(hot_other(h))
                            eng.wait_ge(vec, i * per + (2 * per + per // 2 * h + 1))
                            if more:
                                hot_high(i + 1, h).then_inc(high, 1)
                            own(eng.tensor_reduce(
                                pick[:, h, :, :], prod[:, :, :, :, :].rearrange("p a u n h -> p (a u) h n"), AX.X, ALU.add))
                            summed = n[0]
                            if more:
                                own(hot_own(h))
                            pv = pbk[:, h, 0:HALF * BW].rearrange("p (u c) -> p u c", c=BW)
                            if with_self:
                                own(copy(eng, alpha[:, 4:8, us].rearrange("p h u -> p u h"), pv[:, :, 4:8]))
                            eng.wait_ge(vec, i * per + (2 * per + summed))
                            own(eng.tensor_tensor(alpha[:, 0:4, us].rearrange("p h u -> p u h"), pick[:, h, :, :],
                                                  pv[:, :, 0:4], ALU.add), 1 if more else 3)

                    with eng.Fori(0, TURNS - 1) as i:
                        turn(i, True)
                    turn(TURNS - 1, False)

                @block.tensor
                def _(eng):
                    with eng.Fori(0, TURNS) as i:
                        _, gs = nc.values_load_multi_w_load_instructions(
                            od["gof"][0:1, bass.ds(i * STEP, STEP)], engines=[ENG.PE], min_val=0, max_val=NB,
                            skip_runtime_bounds_check_because="the table is clamped to NB on the chip")
                        for h in range(2):
                            eng.wait_ge(vec, i * per + (per + per // 2 * (h + 1)))
                            for k in range(HALF):
                                e = slice(k * P, (k + 1) * P)
                                for part in range(3):
                                    eng.matmul(pa[:, h, k // QUAD, (k % QUAD) * NB * 4:(k % QUAD + 1) * NB * 4],
                                               hot_o[:, h, e], a_tab[:, part, :, :].rearrange("p n h -> p (n h)"),
                                               start=(part == 0), stop=(part == 2))
                                g = gs[h * HALF + k]
                                for part in range(3):
                                    mm = eng.matmul(pbk[:, h, k * BW:(k + 1) * BW], hot_r[:, h, e],
                                                    b_tab[:, bass.ds(g, 1), part, 0:BW].rearrange("p o c -> p (o c)"),
                                                    start=(part == 0), stop=(part == 2))
                            mm.then_inc(fetched, 1)
            ph.end()

    def softmax(tag, o, H, kind):
        od = order[o]
        HS = 4 if kind != "dot" else 8
        HO = 4 if kind == "weighted" else 8
        S = UC * P
        with ExitStack() as c:
            tbuf = sb(f"sm_t_{tag}", [P, 8, P * UC], F32, c)
            top = alpha[:, 0:HS, :]
            wide = sb(f"sm_wide_{tag}", [P, S], F32, c)
            fill = sb(f"sm_fill_{tag}", [P, 1], F32, c)
            brkc = sb(f"sm_brkc_{tag}", [P, 2, 8], F32, c)
            keyb = sb(f"sm_key_{tag}", [P, S + 2], F32, c)
            wb = sb(f"sm_w_{tag}", [P, S], F32, c)
            brk = sb(f"sm_brk_{tag}", [P, S + 1], F32, c)
            first = sb(f"sm_first_{tag}", [P, S], F32, c)
            col = sb(f"sm_col_{tag}", [P, 2 * HS + 3], F32, c)
            colT = sb(f"sm_colT_{tag}", [8, 3, P + 1], F32, c)
            allT = sb(f"sm_allT_{tag}", [8, 2, P], F32, c)
            carry = sb(f"sm_carry_{tag}", [P, 2, 8], F32, c)
            zt = dram(f"sm_zt_{tag}", [8, UP, P])
            pt = ps(f"sm_pt_{tag}", [P, 4, 512], c)
            ph = Phase()
            turned, copied, stored, loaded, chain, expd, back, tb, cb = (
                ph.sem(n) for n in ("sm_turned", "sm_copied", "sm_stored", "sm_loaded", "sm_chain", "sm_exp", "sm_back", "sm_turned2", "sm_copied2"))
            key_d = od["keyrow"].rearrange("(p r) e -> p (r e)", p=P)
            w_d = od["wrow"].rearrange("(p r) e -> p (r e)", p=P)
            HI = HO if kind != "weighted" else 4
            marks = {}
            with nc.Block() as block:
                @block.vector
                def _(eng):
                    st = Steps(chain)
                    own = lambda ins: st.own(eng, ins)
                    own(eng.memset(fill[:, :], -BIG))
                    own(eng.memset(keyb[:, 0:1], -5.0))
                    own(eng.memset(keyb[:, S + 1:S + 2], -5.0))
                    for k in range(HI * UC):
                        h, j = divmod(k, UC)
                        eng.wait_ge(turned, k + 1)
                        eng.tensor_copy(tbuf[:, h, j * P:(j + 1) * P], pt[:, k % 4, 0:P]).then_inc(copied, 1)
                    eng.wait_ge(loaded, 16 * 4 + 16 * HI)
                    own(eng.tensor_tensor(brk[:, :], keyb[:, 0:S + 1], keyb[:, 1:S + 2], ALU.not_equal))
                    own(eng.tensor_copy(first[:, :], brk[:, 0:S]))
                    own(eng.tensor_scalar(brk[:, :], brk[:, :], -BIG, None, ALU.mult))
                    for w in range(2):
                        own(eng.tensor_reduce(col[:, w:w + 1], brk[:, w:S + w], AX.X, ALU.add))
                        own(eng.tensor_copy(brkc[:, w, :], col[:, w:w + 1].to_broadcast([P, 8])))
                    lg = tbuf[:, 0:HS, :]
                    if kind != "dot":
                        own(eng.scalar_tensor_tensor(out=lg, in0=lg, scalar=0.2, in1=lg, op0=ALU.mult, op1=ALU.max))
                    if kind == "weighted":
                        own(eng.tensor_tensor(lg, lg, wb[:, :].rearrange("p (o s) -> p o s", o=1).to_broadcast([P, HS, S]),
                                              ALU.mult))
                    if kind == "self":
                        own(eng.tensor_tensor(top[:, :, :], lg, tbuf[:, 4:8, :], ALU.max))
                        raw = top
                    else:
                        raw = tbuf
                    for h in range(HS):
                        own(eng.tensor_tensor_scan(top[:, h, :], brk[:, 0:S], raw[:, h, :], -BIG, ALU.add, ALU.max))
                        own(eng.tensor_copy(col[:, 2 + h:3 + h], top[:, h, S - 1:S]))
                    marks["fwd"] = st.n
                    eng.wait_ge(tb, 1)
                    own(eng.tensor_copy(colT[0:HS, 0, 0:P], pt[0:HS, 0, 0:P]))
                    own(eng.tensor_copy(allT[0:HS, 0, :], pt[0:HS, 1, 0:P]))
                    own(eng.memset(colT[0:HS, 1, 0:1], -BIG))
                    own(eng.tensor_tensor_scan(colT[0:HS, 1, 1:P + 1], allT[0:HS, 0, :], colT[0:HS, 0, 0:P], -BIG,
                                               ALU.add, ALU.max))
                    marks["c1"] = st.n
                    eng.wait_ge(tb, 2)
                    own(eng.tensor_copy(carry[:, 0, 0:HS], pt[:, 2, 0:HS]))
                    for h in range(HS):
                        own(eng.tensor_tensor_scan(wide[:, :], brk[:, 0:S], fill[:, 0:1].to_broadcast([P, S]),
                                                   carry[:, 0, h:h + 1], ALU.add, ALU.max))
                        own(eng.tensor_tensor(top[:, h, :], top[:, h, :], wide[:, :], ALU.max))
                        own(eng.tensor_tensor_scan(top[:, h, ::-1], brk[:, S:0:-1], top[:, h, ::-1], -BIG, ALU.add,
                                                   ALU.max))
                        own(eng.tensor_copy(col[:, 2 + h:3 + h], top[:, h, 0:1]))
                    marks["bwd"] = st.n
                    eng.wait_ge(tb, 3)
                    own(eng.tensor_copy(colT[0:HS, 2, 0:P], pt[0:HS, 0, 0:P]))
                    own(eng.tensor_copy(allT[0:HS, 1, :], pt[0:HS, 1, 0:P]))
                    own(eng.memset(colT[0:HS, 1, P:P + 1], -BIG))
                    own(eng.tensor_tensor_scan(colT[0:HS, 1, P - 1::-1], allT[0:HS, 1, ::-1], colT[0:HS, 2, P - 1::-1],
                                               -BIG, ALU.add, ALU.max))
                    marks["c2"] = st.n
                    eng.wait_ge(tb, 4)
                    own(eng.tensor_copy(carry[:, 1, 0:HS], pt[:, 2, 0:HS]))
                    for h in range(HS):
                        own(eng.tensor_tensor_scan(wide[:, ::-1], brk[:, S:0:-1], fill[:, 0:1].to_broadcast([P, S]),
                                                   carry[:, 1, h:h + 1], ALU.add, ALU.max))
                        own(eng.tensor_tensor(top[:, h, :], top[:, h, :], wide[:, :], ALU.max))
                    own(eng.tensor_tensor(lg, lg, top[:, :, :], ALU.subtract))
                    if kind == "self":
                        own(eng.tensor_tensor(tbuf[:, 4:8, :], tbuf[:, 4:8, :], top[:, :, :], ALU.subtract))
                    marks["sub"] = st.n
                    if kind == "self":
                        eng.wait_ge(expd, 1)
                        own(eng.tensor_tensor(tbuf[:, 4:8, :], tbuf[:, 4:8, :],
                                              first[:, :].rearrange("p (o s) -> p o s", o=1).to_broadcast([P, 4, S]),
                                              ALU.mult))
                    marks["exp"] = st.n
                    for k in range(HO * UC):
                        h, j = divmod(k, UC)
                        eng.wait_ge(back, k + 1)
                        eng.tensor_copy(alpha[:, h, j * P:(j + 1) * P], pt[:, k % 4, 0:P]).then_inc(cb, 1)
                    eng.wait_ge(cb, HO * UC)

                @block.scalar
                def _(eng):
                    eng.wait_ge(chain, marks["sub"])
                    eng.activation(tbuf[:, 0:HO, :], tbuf[:, 0:HO, :], ACT.Exp,
                                   scale=float(D // H) ** -0.5 if kind == "dot" else 1.0).then_inc(expd, 1)

                @block.sync
                def _(eng):
                    eng.dma_start(keyb[:, 1:S + 1], key_d).then_inc(loaded, 16)
                    eng.dma_start(wb[:, :], w_d).then_inc(loaded, 16)
                    eng.wait_ge(chain, 3)
                    with nc.allow_non_contiguous_dma(reason="a key from each neighbouring partition"):
                        eng.dma_start(keyb[1:P, 0:1], key_d[0:P - 1, S - 1:S]).then_inc(loaded, 16)
                        eng.dma_start(keyb[0:P - 1, S + 1:S + 2], key_d[1:P, 0:1]).then_inc(loaded, 16)
                    for h in range(HI):
                        eng.wait_ge(copied, UC * (h + 1))
                        eng.dma_start(zt[h, :, :].rearrange("(c p) e -> p c e", p=P),
                                      tbuf[:, h, :].rearrange("p (c e) -> p c e", c=UC)).then_inc(stored, 16)
                    eng.wait_ge(stored, 16 * HI)
                    for h in range(HI):
                        eng.dma_start(tbuf[:, h, :], zt[h, :, :].rearrange("(p r) e -> p (r e)", p=P)).then_inc(loaded, 16)
                    eng.wait_ge(expd, 1)
                    eng.wait_ge(chain, marks["exp"])
                    for h in range(HO):
                        eng.dma_start(zt[h, :, :].rearrange("(p r) e -> p (r e)", p=P), tbuf[:, h, :]).then_inc(stored, 16)
                    eng.wait_ge(stored, 16 * (HI + HO))
                    for h in range(HO):
                        eng.dma_start(tbuf[:, h, :].rearrange("p (c e) -> p c e", c=UC),
                                      zt[h, :, :].rearrange("(c p) e -> p c e", p=P)).then_inc(loaded, 16)
                    eng.wait_ge(loaded, 16 * (4 + HI + HO))

                @block.tensor
                def _(eng):
                    for k in range(HI * UC):
                        h, j = divmod(k, UC)
                        if k >= 4:
                            eng.wait_ge(copied, k - 3)
                        eng.transpose(pt[:, k % 4, 0:P], alpha[:, h, j * P:(j + 1) * P], ident[:, :]).then_inc(turned, 1)
                    eng.wait_ge(copied, HI * UC)
                    for which, (m1, m2) in enumerate((("fwd", "c1"), ("bwd", "c2"))):
                        eng.wait_ge(chain, marks[m1])
                        eng.transpose(pt[0:HS, 0, 0:P], col[:, 2:2 + HS], ident[:, :])
                        eng.transpose(pt[0:HS, 1, 0:P], brkc[:, which, 0:HS], ident[:, :]).then_inc(tb, 1)
                        eng.wait_ge(chain, marks[m2])
                        src = colT[0:HS, 1, 0:P] if which == 0 else colT[0:HS, 1, 1:P + 1]
                        eng.transpose(pt[:, 2, 0:HS], src, ident[0:HS, 0:HS]).then_inc(tb, 1)
                    eng.wait_ge(loaded, 16 * (4 + HI + HO))
                    for k in range(HO * UC):
                        h, j = divmod(k, UC)
                        if k >= 4:
                            eng.wait_ge(cb, k - 3)
                        eng.transpose(pt[:, k % 4, 0:P], tbuf[:, h, j * P:(j + 1) * P], ident[:, :]).then_inc(back, 1)
            ph.end()

    def load_nodes():
        ph = Phase()
        loaded, chain = ph.sem("x_loaded"), ph.sem("x_chain")
        full = N // P
        with nc.Block() as block:
            @block.vector
            def _(eng):
                st = Steps(chain)
                st.own(eng, eng.memset(x_sb[:, NB - 1, :], 0.0))
                st.own(eng, eng.memset(b_tab[:, :, :, :], 0.0))
                st.own(eng, eng.memset(alpha[:, :, :], 0.0))

            @block.sync
            def _(eng):
                eng.dma_start(x_sb[:, 0:full, :], x_in[0:full * P, :].rearrange("(b p) d -> p b d", p=P))\
                    .then_inc(loaded, 16)
                eng.wait_ge(chain, 1)
                eng.dma_start(x_sb[0:N - full * P, full, :], x_in[full * P:N, :]).then_inc(loaded, 16)
                eng.wait_ge(loaded, 32)
        ph.end()

    def gather_loop(eng, od, table, ring, idx, copied, seen, landed, vec, per, free_at):
        with eng.Fori(0, TURNS) as i:
            for q in range(STEP // QUAD):
                eng.wait_ge(vec, i * per + free_at[q])
                eng.sem_inc(seen, 1)
                eng.tensor_copy(idx[:, q * QUAD:(q + 1) * QUAD], od["oth"][:, bass.ds(i * STEP + q * QUAD, QUAD)])\
                    .then_inc(copied, 1)
                eng.wait_ge(copied, i * (STEP // QUAD) + q + 1)
                eng.sem_inc(seen, 1)
                for k in range(q * QUAD, (q + 1) * QUAD):
                    eng.indirect_dma_start(out=ring[:, k, :], out_offset=None, in_=table,
                                           in_offset=bass.IndirectOffsetOnAxis(ap=idx[:, k:k + 1], axis=0))\
                        .then_inc(landed[k], 16)

    def feed_indices(eng, od, idx, copied, seen, vec, per, free_at):
        with eng.Fori(0, TURNS) as i:
            for h in range(2):
                eng.wait_ge(vec, i * per + free_at[h])
                eng.sem_inc(seen, 1)
                eng.activation(idx[:, h * HALF:(h + 1) * HALF], od["oth"][:, bass.ds(i * STEP + h * HALF, HALF)], ACT.Copy)\
                    .then_inc(copied, 1)

    def gather_fed(eng, table, ring, idx, copied, told, landed):
        with eng.Fori(0, TURNS) as i:
            for h in range(2):
                eng.wait_ge(copied, i * 2 + h + 1)
                eng.sem_inc(told, 1)
                for k in range(h * HALF, (h + 1) * HALF):
                    eng.indirect_dma_start(out=ring[:, k, :], out_offset=None, in_=table,
                                           in_offset=bass.IndirectOffsetOnAxis(ap=idx[:, k:k + 1], axis=0))\
                        .then_inc(landed[k], 16)

    def adder(eng, i, n, per, vec, gs, own, sums, out_ps, width, wait_mm):
        last = {0: -1, 1: 0}

        def add(q):
            for j in range(QUAD):
                wait_mm(q * QUAD + j)
                eng.wait_ge(vec, i * per + (per + last[j % 2]))
                g = bass.ds(gs[q * QUAD + j], 1)
                to = sums[j % 2][:, g, 0:width]
                own(eng.tensor_tensor(to, to, out_ps(q, j), ALU.add), False)
                last[j % 2] = n[0]
        return add

    def join_sums(eng, vec, per, sums, width):
        eng.wait_ge(vec, (TURNS + 1) * per)
        eng.tensor_tensor(sums[0][:, :, 0:width], sums[0][:, :, 0:width], sums[1][:, :, 0:width], ALU.add).then_inc(vec, 1)
        eng.wait_ge(vec, (TURNS + 1) * per + 1)

    def aggregate(tag, o, table, H, extra):
        od = order[o]
        W = D + extra
        F = D // H
        per = QUAD * 7
        after = {0: 3, 1: 6, 2: 13, 3: 20}
        with ExitStack() as c:
            ring = sb(f"ag_ring_{tag}", [P, STEP, D], F32, c)
            idx = sb(f"ag_idx_{tag}", [P, STEP], U32, c)
            hot = sb(f"ag_hot_{tag}", [P, 2, QUAD, P], F32, c)
            rows = sb(f"ag_rows_{tag}", [P, 2, QUAD, W], F32, c)
            acc_odd = sb(f"ag_odd_{tag}", [P, GX, W], F32, c)
            sums = (acc, acc_odd)
            po = ps(f"ag_po_{tag}", [P, 8, 512], c)
            ph = Phase()
            seen, told = ph.sem("ag_seen"), ph.sem("ag_told")
            landed = [ph.sem(f"ag_landed{k}") for k in range(STEP)]
            vec, summed, copied = ph.sem("ag_vector"), ph.sem("ag_summed"), ph.sem("ag_idx_copied")
            with nc.Block() as block:
                @block.gpsimd
                def _(eng):
                    gather_fed(eng, table, ring, idx, copied, told, landed)

                @block.scalar
                def _(eng):
                    feed_indices(eng, od, idx, copied, seen, vec, per, (after[1] - 1, after[3] - 1))

                @block.vector
                def _(eng):
                    eng.memset(acc[:, :, :], 0.0).then_inc(vec, per - 1)
                    eng.memset(acc_odd[:, :, :], 0.0).then_inc(vec, 1)
                    eng.wait_ge(vec, per)
                    with eng.Fori(0, TURNS) as i:
                        n = [0]
                        _, gs = nc.values_load_multi_w_load_instructions(
                            od["gof"][0:1, bass.ds(i * STEP, STEP)], engines=[ENG.DVE], min_val=0, max_val=NB,
                            skip_runtime_bounds_check_because="the table is clamped to NB on the chip")

                        def own(ins, wait=True):
                            ins.then_inc(vec, 1)
                            n[0] += 1
                            if wait:
                                eng.wait_ge(vec, i * per + (per + n[0]))

                        def prepare(q):
                            us = bass.ds(i * STEP + q * QUAD, QUAD)
                            own(eng.tensor_tensor(
                                hot[:, q % 2, :, :], iota_row[:, :].rearrange("p (o n) -> p o n", o=1).to_broadcast([P, QUAD, P]),
                                od["rel"][:, us].rearrange("p (u o) -> p u o", o=1).to_broadcast([P, QUAD, P]),
                                ALU.is_equal), False)
                            for j in range(QUAD):
                                eng.wait_ge(landed[q * QUAD + j], i * 16 + 16)
                            own(eng.tensor_tensor(
                                rows[:, q % 2, :, 0:D].rearrange("p u (h f) -> p u h f", h=H),
                                ring[:, q * QUAD:(q + 1) * QUAD, :].rearrange("p u (h f) -> p u h f", h=H),
                                alpha[:, 0:H, us].rearrange("p h u -> p u h").rearrange("p u (h o) -> p u h o", o=1)
                                .to_broadcast([P, QUAD, H, F]), ALU.mult), False)
                            own(eng.tensor_copy(rows[:, q % 2, :, D:W], alpha[:, 0:extra, us].rearrange("p h u -> p u h")),
                                False)

                        add = adder(eng, i, n, per, vec, gs, own, sums,
                                    lambda q, j: po[:, (q % 2) * QUAD + j:(q % 2) * QUAD + j + 1, 0:W], W,
                                    lambda u: eng.wait_ge(summed, i * STEP + u + 1))
                        prepare(0)
                        prepare(1)
                        add(0)
                        prepare(2)
                        add(1)
                        prepare(3)
                        add(2)
                        add(3)
                    join_sums(eng, vec, per, sums, W)

                @block.tensor
                def _(eng):
                    with eng.Fori(0, TURNS) as i:
                        for q in range(STEP // QUAD):
                            eng.wait_ge(vec, i * per + (per + after[q]))
                            for j in range(QUAD):
                                eng.matmul(po[:, (q % 2) * QUAD + j, 0:W], hot[:, q % 2, j, :], rows[:, q % 2, j, :],
                                           start=True, stop=True).then_inc(summed, 1)
            ph.end()

    def scores_dot(tag, o, table, k_split, H):
        od = order[o]
        F = D // H
        per = 10
        with ExitStack() as c:
            ring = sb(f"sd_ring_{tag}", [P, STEP, D], F32, c)
            idx = sb(f"sd_idx_{tag}", [P, STEP], U32, c)
            rows_r = sb(f"sd_rr_{tag}", [P, 2, HALF * P], BF16, c)
            hot = sb(f"sd_hot_{tag}", [P, 2, HALF * P], BF16, c)
            prod = sb(f"sd_prod_{tag}", [P, QUAD, D], F32, c)
            pk = ps(f"sd_pk_{tag}", [P, 8, 512], c)
            ph = Phase()
            seen, told = ph.sem("sd_seen"), ph.sem("sd_told")
            landed = [ph.sem(f"sd_landed{k}") for k in range(STEP)]
            rowin = [ph.sem(f"sd_rows{h}") for h in range(2)]
            vec, spread, copied = ph.sem("sd_vector"), ph.sem("sd_spread"), ph.sem("sd_idx_copied")
            with nc.Block() as block:
                @block.sync
                def _(eng):
                    with eng.Fori(0, TURNS) as i:
                        for h in range(2):
                            eng.wait_ge(vec, i * per + h + 1)
                            eng.dma_start(rows_r[:, h, :], od["relrow"][bass.ds(i * STEP + h * HALF, HALF), :]
                                          .rearrange("(o t) e -> o (t e)", o=1).to_broadcast([P, HALF * P]))\
                                .then_inc(rowin[h], 16)

                @block.gpsimd
                def _(eng):
                    gather_fed(eng, table, ring, idx, copied, told, landed)

                @block.scalar
                def _(eng):
                    feed_indices(eng, od, idx, copied, seen, vec, per, (5, 9))

                @block.vector
                def _(eng):
                    eng.sem_inc(vec, per)
                    with eng.Fori(0, TURNS) as i:
                        n = [0]

                        def own(ins, wait=True):
                            ins.then_inc(vec, 1)
                            n[0] += 1
                            if wait:
                                eng.wait_ge(vec, i * per + (per + n[0]))

                        for h in range(2):
                            eng.wait_ge(rowin[h], i * 16 + 16)
                            own(eng.tensor_scalar(hot[:, h, :], rows_r[:, h, :], iota_col[:, :], None, ALU.is_equal), False)
                        for q in range(STEP // QUAD):
                            us = bass.ds(i * STEP + q * QUAD, QUAD)
                            for j in range(QUAD):
                                eng.wait_ge(landed[q * QUAD + j], i * 16 + 16)
                            eng.wait_ge(spread, i * 4 + q + 1)
                            own(eng.tensor_tensor(prod[:, :, :], ring[:, q * QUAD:(q + 1) * QUAD, :],
                                                  pk[:, (q % 2) * QUAD:(q % 2 + 1) * QUAD, 0:D], ALU.mult))
                            own(eng.tensor_reduce(alpha[:, 0:H, us].rearrange("p h u -> p u h"),
                                                  prod[:, :, :].rearrange("p u (h f) -> p u h f", h=H), AX.X, ALU.add))

                @block.tensor
                def _(eng):
                    with eng.Fori(0, TURNS) as i:
                        _, gs = nc.values_load_multi_w_load_instructions(
                            od["gof"][0:1, bass.ds(i * STEP, STEP)], engines=[ENG.PE], min_val=0, max_val=NB,
                            skip_runtime_bounds_check_because="the table is clamped to NB on the chip")
                        for q in range(STEP // QUAD):
                            eng.wait_ge(vec, i * per + (per + (1, 2, 3, 5)[q]))
                            for j in range(QUAD):
                                u = q * QUAD + j
                                e = slice((u % HALF) * P, (u % HALF + 1) * P)
                                for part in range(3):
                                    mm = eng.matmul(pk[:, (q % 2) * QUAD + j, 0:D], hot[:, u // HALF, e],
                                                    k_split[:, bass.ds(gs[u], 1), part, :].rearrange("p o n -> p (o n)"),
                                                    start=(part == 0), stop=(part == 2))
                            mm.then_inc(spread, 1)
            ph.end()

    def aggregate_edges(tag, o, table, we_ap):
        od = order[o]
        per = QUAD * 6
        hot_at = {0: 1, 1: 3, 2: 9, 3: 15}
        with ExitStack() as c:
            ring = sb(f"ae_ring_{tag}", [P, STEP, D], F32, c)
            idx = sb(f"ae_idx_{tag}", [P, STEP], U32, c)
            feat = sb(f"ae_feat_{tag}", [P, STEP, DE], F32, c)
            featT = sb(f"ae_featT_{tag}", [DE, 2, QUAD, P], F32, c)
            We = sb(f"ae_we_{tag}", [DE, D], F32, c)
            hot = sb(f"ae_hot_{tag}", [P, 2, QUAD, P], F32, c)
            pre = sb(f"ae_pre_{tag}", [P, 2, QUAD, D], F32, c)
            msg = sb(f"ae_msg_{tag}", [P, 2, QUAD, D], F32, c)
            acc_odd = sb(f"ae_odd_{tag}", [P, GX, D], F32, c)
            sums = (acc, acc_odd)
            pT = ps(f"ae_pT_{tag}", [P, 2, QUAD * P], c)
            pM = ps(f"ae_pM_{tag}", [P, 2, 512], c)
            po = ps(f"ae_po_{tag}", [P, 4, 512], c)
            ph = Phase()
            seen = ph.sem("ae_seen")
            told, warmed = ph.sem("ae_told"), ph.sem("ae_warmed")
            landed = [ph.sem(f"ae_landed{k}") for k in range(STEP)]
            featin = [ph.sem(f"ae_featin{h}") for h in range(4)]
            wl, vec, mapped, summed, turned, copied, evac, msgs = (ph.sem(n) for n in (
                "ae_weights", "ae_vector", "ae_mapped", "ae_summed", "ae_turned", "ae_idx_copied", "ae_featT", "ae_msgs"))
            with nc.Block() as block:
                @block.gpsimd
                def _(eng):
                    gather_loop(eng, od, table, ring, idx, copied, seen, landed, vec, per, (2, 4, 10, 16))

                @block.sync
                def _(eng):
                    eng.dma_start(We[:, :], we_ap).then_inc(wl, 16)
                    with eng.Fori(0, TURNS) as i:
                        _, ts = nc.values_load_multi_w_load_instructions(
                            od["tof"][0:1, bass.ds(i * STEP, STEP)], engines=[ENG.SP], min_val=0, max_val=T - 1,
                            skip_runtime_bounds_check_because="the table holds tiles, 0 to T - 1")
                        for q in range(STEP // QUAD):
                            eng.wait_ge(turned, i * 4 + q + 1)
                            for j in range(QUAD):
                                u = q * QUAD + j
                                eng.dma_start(feat[:, u, :], attr_pad.rearrange("(t e) d -> t e d", e=P)
                                              [bass.ds(ts[u], 1), :, :].rearrange("o e d -> e (o d)"))\
                                    .then_inc(featin[q], 16)

                @block.scalar
                def _(eng):
                    eng.activation(msg[:, 0, 0, 0:1], eps[:, :], ACT.Silu).then_inc(warmed, 1)
                    eng.wait_ge(warmed, 1)
                    with eng.Fori(0, TURNS) as i:
                        def evacuate(q):
                            eng.wait_ge(turned, i * 4 + q + 5)
                            eng.activation(featT[:, q % 2, :, :].rearrange("p u e -> p (u e)"), pT[0:DE, q % 2, :], ACT.Copy)\
                                .then_inc(evac, 1)

                        def silu(q):
                            eng.wait_ge(vec, i * per + (per + hot_at[q] + 1))
                            eng.activation(msg[:, q % 2, :, :], pre[:, q % 2, :, :], ACT.Silu).then_inc(msgs, 1)

                        evacuate(0)
                        evacuate(1)
                        silu(0)
                        evacuate(2)
                        silu(1)
                        evacuate(3)
                        silu(2)
                        silu(3)

                @block.vector
                def _(eng):
                    eng.memset(acc[:, :, :], 0.0).then_inc(vec, per - 1)
                    eng.memset(acc_odd[:, :, :], 0.0).then_inc(vec, 1)
                    eng.wait_ge(vec, per)
                    with eng.Fori(0, TURNS) as i:
                        n = [0]
                        _, gs = nc.values_load_multi_w_load_instructions(
                            od["gof"][0:1, bass.ds(i * STEP, STEP)], engines=[ENG.DVE], min_val=0, max_val=NB,
                            skip_runtime_bounds_check_because="the table is clamped to NB on the chip")

                        def own(ins, wait=True):
                            ins.then_inc(vec, 1)
                            n[0] += 1
                            if wait:
                                eng.wait_ge(vec, i * per + (per + n[0]))

                        def prepare(q):
                            us = bass.ds(i * STEP + q * QUAD, QUAD)
                            own(eng.tensor_tensor(
                                hot[:, q % 2, :, :], iota_row[:, :].rearrange("p (o n) -> p o n", o=1).to_broadcast([P, QUAD, P]),
                                od["rel"][:, us].rearrange("p (u o) -> p u o", o=1).to_broadcast([P, QUAD, P]),
                                ALU.is_equal), False)
                            for j in range(QUAD):
                                eng.wait_ge(landed[q * QUAD + j], i * 16 + 16)
                            eng.wait_ge(mapped, i * 4 + q + 1)
                            own(eng.tensor_tensor(
                                pre[:, q % 2, :, :].rearrange("p (a u) f -> p a (u f)", a=2),
                                ring[:, q * QUAD:(q + 1) * QUAD, :].rearrange("p (a u) f -> p a (u f)", a=2),
                                pM[:, :, :], ALU.add), False)

                        add = adder(eng, i, n, per, vec, gs, own, sums,
                                    lambda q, j: po[:, (q % 2) * 2 + j // 2:(q % 2) * 2 + j // 2 + 1,
                                                    (j % 2) * D:(j % 2 + 1) * D], D,
                                    lambda u: eng.wait_ge(summed, i * STEP + (u | 1) + 1))
                        prepare(0)
                        prepare(1)
                        add(0)
                        prepare(2)
                        add(1)
                        prepare(3)
                        add(2)
                        add(3)
                    join_sums(eng, vec, per, sums, D)

                @block.tensor
                def _(eng):
                    eng.wait_ge(wl, 16)
                    eng.sem_inc(turned, 4)

                    def turn(i, q):
                        eng.wait_ge(featin[q], i * 64 + 64)
                        eng.sem_inc(told, 1)
                        for j in range(QUAD):
                            mm = eng.transpose(pT[0:DE, q % 2, j * P:(j + 1) * P], feat[:, q * QUAD + j, :], ident[:, :])
                        mm.then_inc(turned, 1)

                    def project(i, q):
                        eng.wait_ge(evac, i * 4 + q + 1)
                        eng.wait_ge(vec, i * per + (16, per + 2, per + 4, per + 10)[q])
                        for j in range(QUAD):
                            mm = eng.matmul(pM[:, j // 2, (j % 2) * D:(j % 2 + 1) * D], featT[:, q % 2, j, :], We[:, :],
                                            start=True, stop=True)
                        mm.then_inc(mapped, 1)

                    def reduce(i, q):
                        eng.wait_ge(msgs, i * 4 + q + 1)
                        for j in range(QUAD):
                            eng.matmul(po[:, (q % 2) * 2 + j // 2, (j % 2) * D:(j % 2 + 1) * D], hot[:, q % 2, j, :],
                                       msg[:, q % 2, j, :], start=True, stop=True).then_inc(summed, 1)

                    def one_turn(i, more):
                        project(i, 0)
                        project(i, 1)
                        turn(i, 2)
                        reduce(i, 0)
                        project(i, 2)
                        turn(i, 3)
                        reduce(i, 1)
                        project(i, 3)
                        if more:
                            turn(i + 1, 0)
                            turn(i + 1, 1)
                        reduce(i, 2)
                        reduce(i, 3)

                    turn(0, 0)
                    turn(0, 1)
                    with eng.Fori(0, TURNS - 1) as i:
                        one_turn(i, True)
                    one_turn(TURNS - 1, False)
            ph.end()

    def bc(ap, shape):
        return ap.to_broadcast(shape)

    def finish(tag, kind, vecs=(), guard=0.0):
        H = 8 if kind == "dot_add" else 4
        F = D // H
        with ExitStack() as c:
            B = sb(f"fi_b_{tag}", [P, max(1, len(vecs)), D], F32, c)
            s = sb(f"fi_s_{tag}", [P, NB, 8], F32, c)
            r = sb(f"fi_r_{tag}", [P, NB, 8], F32, c)
            iso = sb(f"fi_iso_{tag}", [P, NB, 4], F32, c)
            st6 = sb(f"fi_st_{tag}", [P, NB, 6], F32, c)
            mv = sb(f"fi_mv_{tag}", [P, NB, 2], F32, c)
            rstd = sb(f"fi_rs_{tag}", [P, NB], F32, c)
            e3 = sb(f"fi_e3_{tag}", [P, 1], F32, c)
            ph = Phase()
            loaded, chain, rooted = ph.sem("fi_loaded"), ph.sem("fi_chain"), ph.sem("fi_rooted")
            mark = {}
            with nc.Block() as block:
                @block.sync
                def _(eng):
                    for j, v in enumerate(vecs):
                        eng.dma_start(B[:, j, :], v.to_broadcast([P, D])).then_inc(loaded, 16)

                @block.vector
                def _(eng):
                    st = Steps(chain)
                    own = lambda ins: st.own(eng, ins)
                    A = acc[:, 0:NB, 0:D]
                    Ah = A.rearrange("p b (h f) -> p b h f", h=H)
                    heads = lambda ap: ap.rearrange("p b (h o) -> p b h o", o=1).to_broadcast([P, NB, H, F])
                    rowsof = lambda j: B[:, j:j + 1, :].to_broadcast([P, NB, D])
                    if vecs:
                        eng.wait_ge(loaded, 16 * len(vecs))
                    if kind in ("gat", "gat_add"):
                        own(eng.tensor_scalar(iso[:, :, :], acc[:, 0:NB, D:D + 4], 0.0, None, ALU.is_equal))
                        own(eng.tensor_tensor(r[:, :, 0:4], acc[:, 0:NB, D + 4:D + 8], iso[:, :, :], ALU.max))
                        own(eng.scalar_tensor_tensor(out=s[:, :, 0:4], in0=acc[:, 0:NB, D:D + 4], scalar=guard,
                                                     in1=r[:, :, 0:4], op0=ALU.add, op1=ALU.add))
                        own(eng.reciprocal(s[:, :, 0:4], s[:, :, 0:4]))
                        own(eng.tensor_tensor(r[:, :, 0:4], r[:, :, 0:4], s[:, :, 0:4], ALU.mult))
                        hb = node_a[:, :, :].rearrange("p b (h f) -> p b h f", h=H)
                        own(eng.tensor_tensor(Ah, Ah, heads(s[:, :, 0:4]), ALU.mult))
                        own(eng.tensor_tensor(hb, hb, heads(r[:, :, 0:4]), ALU.mult))
                        own(eng.tensor_tensor(A, A, rowsof(0), ALU.add))
                        own(eng.tensor_tensor(node_a[:, :, :], A, node_a[:, :, :], ALU.add))
                        if kind == "gat_add":
                            own(eng.tensor_tensor(x_sb[:, :, :], x_sb[:, :, :], node_a[:, :, :], ALU.add))
                    elif kind in ("dot_add", "relu_add"):
                        own(eng.tensor_scalar(s[:, :, 0:H], acc[:, 0:NB, D:D + H], guard, None, ALU.max))
                        own(eng.reciprocal(s[:, :, 0:H], s[:, :, 0:H]))
                        own(eng.tensor_tensor(Ah, Ah, heads(s[:, :, 0:H]), ALU.mult))
                        if kind == "relu_add":
                            own(eng.tensor_tensor(A, A, rowsof(0), ALU.add))
                            own(eng.scalar_tensor_tensor(out=x_sb[:, :, :], in0=A, scalar=0.0, in1=x_sb[:, :, :],
                                                         op0=ALU.max, op1=ALU.add))
                        else:
                            own(eng.tensor_tensor(x_sb[:, :, :], x_sb[:, :, :], A, ALU.add))
                    else:
                        own(eng.memset(e3[:, :], 1e-3))
                        for b in range(NB):
                            own(eng.bn_stats(st6[:, b, :], acc[:, b, 0:D]))
                            own(eng.bn_aggr(mv[:, b, :], st6[:, b, :]))
                        mark["var"] = st.n
                        eng.wait_ge(rooted, 1)
                        own(eng.reciprocal(rstd[:, :], rstd[:, :]))
                        own(eng.tensor_tensor(A, A, mv[:, :, 0:1].to_broadcast([P, NB, D]), ALU.subtract))
                        own(eng.tensor_tensor(A, A, rstd[:, :].rearrange("p (b o) -> p b o", o=1).to_broadcast([P, NB, D]),
                                              ALU.mult))
                        own(eng.tensor_tensor(A, A, rowsof(0), ALU.mult))
                        own(eng.tensor_tensor(A, A, rowsof(1), ALU.add))
                        own(eng.tensor_tensor(x_sb[:, :, :], x_sb[:, :, :], A, ALU.add))

                @block.scalar
                def _(eng):
                    if kind == "edge_add":
                        eng.wait_ge(chain, mark["var"])
                        eng.activation(rstd[:, :], mv[:, :, 1], ACT.Sqrt, bias=e3[:, :]).then_inc(rooted, 1)
            ph.end()

    def store_nodes():
        ph = Phase()
        full = N // P
        written = ph.sem("out_written")
        with nc.Block() as block:
            @block.sync
            def _(eng):
                eng.dma_start(out[0:full * P, :].rearrange("(b p) d -> p b d", p=P), x_sb[:, 0:full, :]).then_inc(written, 16)
                eng.dma_start(out[full * P:N, :], x_sb[0:N - full * P, full, :]).then_inc(written, 16)
                eng.wait_ge(written, 32)
        nc.all_engine_barrier()

    setup()
    records()
    sort_by_source()
    units("d")
    units("s")
    x_sb = sb("x_sb", [P, NB, D])
    node_a = sb("node_a", [P, NB, D])
    acc = sb("acc", [P, GX, ACCW])
    alpha = sb("alpha", [P, 8, UP])
    a_tab = sb("a_tab", [P, 3, NB, 4], BF16)
    b_tab = sb("b_tab", [P, GX, 3, 8], BF16)
    score_own = sb("score_own", [P, NB, 8])
    self_log = sb("self_log", [P, NB, 4])

    row = lambda v: v.rearrange("(o f) -> o f", o=1)
    whole = lambda w: [(lambda W: W[:, :, :], w.rearrange("(k p) n -> p k n", p=P))]
    load_nodes()
    stage = [0]

    def go(f, *args, **kw):
        stage[0] += 1
        if stage[0] <= upto:
            f(*args, **kw)

    for tag, W, vs, vd, b, norm, kind in (("0a", W1, as1, ad1, b1, True, "gat"), ("0b", W2, as2, ad2, b2, False, "gat_add")):
        go(dense, tag, x_sb if norm else node_a, norm, [node_a], whole(W), scores=(vs, vd), stores=[(node_a, tab_a)])
        go(score_tables, tag, True, 0, 4)
        go(scores_gat, tag, "d", True)
        go(softmax, tag, "d", 4, "self")
        go(aggregate, tag, "d", tab_a, 4, 8)
        go(finish, tag, kind, [row(b)], 1e-16)

    with ExitStack() as c:
        k_split = sb("k_split", [P, GX, 3, D], BF16, c)
        third = lambda m: (lambda W: W[:, :, m * D:(m + 1) * D])
        go(dense, "1", x_sb, True, [node_a, acc[:, 0:NB, 0:D], None],
           [(third(m), w.rearrange("(k p) n -> p k n", p=P)) for m, w in enumerate((Wq, Wv, Wk))],
           b_aps=(bq, bv, bk), k_split=k_split, stores=[(node_a, tab_a), (acc[:, 0:NB, 0:D], tab_b)])
        go(scores_dot, "1", "d", tab_a, k_split, 8)
    go(softmax, "1", "d", 8, "dot")
    go(aggregate, "1", "d", tab_b, 8, 8)
    go(finish, "1", "dot_add", [], 1e-16)

    go(dense, "2", x_sb, True, [node_a], [(lambda W: W[:, :, :], L2W[0:D, :].rearrange("(k p) n -> p k n", p=P))],
       b_aps=(L2b,), stores=[(node_a, tab_a)])
    go(aggregate_edges, "2", "d", tab_a, L2W[D:D + DE, :])
    go(finish, "2", "edge_add", [row(L2g), row(L2be)])

    go(dense, "3", x_sb, True, [node_a],
       [(lambda W, h=h: W[:, :, h * DE:(h + 1) * DE], L3W[h, :, :].rearrange("(k p) n -> p k n", p=P)) for h in range(4)],
       scores=(L3as, L3an), stores=[(node_a, tab_a)])
    go(score_tables, "3", False, 4, 0)
    go(scores_gat, "3", "s", False)
    go(softmax, "3", "s", 4, "weighted")
    go(aggregate, "3", "s", tab_a, 4, 4)
    go(finish, "3", "relu_add", [L3b.rearrange("(o h) f -> o (h f)", o=1)], 1e-30)
    if dumps is not None:
        dumps(locals())
    store_nodes()
    ctx.close()


_INS = ["x", "src", "dst", "edge_attr_64", "edge_weight", "L0_gnn_W1", "L0_gnn_att_src1", "L0_gnn_att_dst1", "L0_gnn_b1",
        "L0_gnn_W2", "L0_gnn_att_src2", "L0_gnn_att_dst2", "L0_gnn_b2", "L1_gnn_Wq", "L1_gnn_bq", "L1_gnn_Wk", "L1_gnn_bk",
        "L1_gnn_Wv", "L1_gnn_bv", "L2_gnn_W", "L2_gnn_b", "L2_gnn_gamma", "L2_gnn_beta", "L3_gnn_W", "L3_gnn_a_self",
        "L3_gnn_a_neigh", "L3_gnn_bias"]


def kernel(**inputs):
    import numpy as np
    import concourse.bacc as bacc
    from concourse.bass_utils import run_bass_kernel_spmd

    nc = bacc.Bacc("TRN2", target_bir_lowering=False, num_devices=1)
    arrays, args = {}, []
    for name in _INS:
        a = np.ascontiguousarray(inputs[name])
        arrays[f"in_{name}_dram"] = a
        args.append(nc.dram_tensor(f"in_{name}_dram", a.shape, mybir.dt.from_np(a.dtype), kind="ExternalInput").ap())
    out = nc.dram_tensor("out_dram", (N, D), F32, kind="ExternalOutput").ap()
    gnn_kernel(nc, *args, out)
    r = run_bass_kernel_spmd(nc, [arrays], core_ids=[0])
    return r.results[0]["out_dram"]
```
